# Optimizing a Trainium2 kernel written in Bass

```python
import numpy as np
import jax
import jax.numpy as jnp

def _softmax(x, axis=-1):
    return jax.nn.softmax(x, axis=axis)

def _gelu(x):
    return jax.nn.gelu(x, approximate=True)

def _silu(x):
    return jax.nn.silu(x)

def _sigmoid(x):
    return jax.nn.sigmoid(x)

def _layernorm(x, axis=-1, eps=1e-05):
    m = jnp.mean(x, axis=axis, keepdims=True)
    v = jnp.var(x, axis=axis, keepdims=True)
    return (x - m) / jnp.sqrt(v + eps)

def _scatter_add(tgt, idx, src, axis=0):
    return tgt.at[idx].add(src)

def _segment_sum(src, seg, n):
    return jax.ops.segment_sum(src, seg, n)
kernel_name = 'mk_gnn_ffn_d1_gnn_r8_7d7b9e'

def setup_inputs(seed: int=0):
    np.random.seed(seed)
    _w = jnp.asarray

    def _rec_inputs():
        import jax
        import jax.numpy as jnp
        _gk = jax.random.key(seed)
        x = -6.415e-05 + 1 * jax.random.normal(jax.random.fold_in(_gk, 1), (2500, 512), jnp.float32)
        src = jax.random.randint(jax.random.fold_in(_gk, 2), (80000,), 0, 2500, jnp.int32)
        dst = jnp.minimum((2500 * jax.random.uniform(jax.random.fold_in(_gk, 3), (80000,)) ** 2.0).astype(jnp.int32), 19999)
        _o = jnp.argsort(dst, stable=True)
        src = src[_o]
        dst = dst[_o]
        edge_type_8 = jax.random.randint(jax.random.fold_in(_gk, 12), (80000,), 0, 8, jnp.int32)
        return (x, src, dst, edge_type_8)
    x, src, dst, edge_type_8 = _rec_inputs()

    def _L0_gnn_setup():
        import jax, jax.numpy as jnp
        import numpy as np
        N = 2500
        E = 20000
        D = 512
        R = 8
        key = jax.random.key(seed)
        ks = jax.random.split(key, 8)
        inp = {'input': jax.random.normal(ks[0], (N, D), dtype=jnp.float32), 'heads': jax.random.randint(ks[1], (E,), 0, N), 'tails': jax.random.randint(ks[2], (E,), 0, N), 'rel': jax.random.randint(ks[3], (E,), 0, R), 'W_self': jax.random.normal(ks[4], (D, D), dtype=jnp.float32) * 0.03, 'b_self': jnp.zeros((D,), dtype=jnp.float32), 'W_rel': jax.random.normal(ks[5], (2 * R, D, D), dtype=jnp.float32) * 0.03, 'b_rel': jnp.zeros((2 * R, D), dtype=jnp.float32)}
        return inp
    _L0_gnn_all = _L0_gnn_setup()
    _L0_gnn_in = {k: v for k, v in _L0_gnn_all.items() if k in ('W_self', 'b_self', 'W_rel', 'b_rel')}
    del _L0_gnn_all

    def _L0_ffn_setup():
        import jax, jax.numpy as jnp
        import numpy as np
        BINS = jnp.array([-1.5, -1.0, -0.5, 0.0, 0.5, 1.0, 1.5], dtype=jnp.float32)
        N_BINS = BINS.shape[0] + 1
        INDEX = 0
        key = jax.random.key(seed)
        k1, k2 = jax.random.split(key)
        x = jax.random.normal(k1, (8, 512, 512), dtype=jnp.float32)
        W = jax.random.normal(k2, (N_BINS, 512, 512), dtype=jnp.float32) * 0.02
        return {'x': x, 'W': W}
    _L0_ffn_all = _L0_ffn_setup()
    _L0_ffn_in = {k: v for k, v in _L0_ffn_all.items() if k in ('W',)}
    del _L0_ffn_all
    return {'x': x, 'src': src, 'dst': dst, 'edge_type_8': edge_type_8, 'L0_gnn_W_self': _L0_gnn_in['W_self'], 'L0_gnn_b_self': _L0_gnn_in['b_self'], 'L0_gnn_W_rel': _L0_gnn_in['W_rel'], 'L0_gnn_b_rel': _L0_gnn_in['b_rel'], 'L0_ffn_W': _L0_ffn_in['W']}

def reference(x, src, dst, edge_type_8, L0_gnn_W_self, L0_gnn_b_self, L0_gnn_W_rel, L0_gnn_b_rel, L0_ffn_W):
    import jax
    import jax.numpy as jnp

    def _L0_gnn_ref(input, heads, tails, rel, W_self, b_self, W_rel, b_rel):
        import jax, jax.numpy as jnp
        import numpy as np
        N = 2500
        E = 20000
        D = 512
        R = 8
        h_self = input @ W_self.T + b_self
        H_all = jnp.einsum('rod,nd->rno', W_rel, input) + b_rel[:, None, :]
        msg_to_heads = H_all[rel, tails]
        msg_to_tails = H_all[rel + R, heads]
        agg = jax.ops.segment_sum(msg_to_heads, heads, num_segments=N) + jax.ops.segment_sum(msg_to_tails, tails, num_segments=N)
        return jax.nn.relu(h_self + agg)

    def _L0_ffn_ref(x, W):
        import jax, jax.numpy as jnp
        import numpy as np
        BINS = jnp.array([-1.5, -1.0, -0.5, 0.0, 0.5, 1.0, 1.5], dtype=jnp.float32)
        N_BINS = BINS.shape[0] + 1
        INDEX = 0
        y = x[..., INDEX]
        mem = jnp.sum(y[..., None] > BINS, axis=-1)
        B, T, D = x.shape
        xf = x.reshape(B * T, D)
        memf = mem.reshape(B * T)
        out = jnp.zeros((B * T, W.shape[-1]), dtype=x.dtype)
        for k in range(N_BINS):
            sel = (memf == k)[:, None].astype(x.dtype)
            out = out + sel * (xf @ W[k])
        return out.reshape(B, T, W.shape[-1])
    x = x + _L0_gnn_ref(_layernorm(x, axis=-1), src, dst, edge_type_8, L0_gnn_W_self, L0_gnn_b_self, L0_gnn_W_rel, L0_gnn_b_rel)
    x = x + _L0_ffn_ref(_layernorm(x, axis=-1)[None], L0_ffn_W)[0]
    return x

_drawn_inputs = setup_inputs


def setup_inputs(seed=0):
    import zlib

    import numpy as np

    out = dict(_drawn_inputs(seed))
    spreads = {'L0_gnn_b_self': (0.0, 0.34), 'L0_gnn_b_rel': (0.0, 0.1)}
    factors = {}
    for name, (base, spread) in spreads.items():
        noise = np.random.default_rng([zlib.crc32(name.encode()), seed]).standard_normal(out[name].shape)
        drawn = base * np.exp(spread * noise) if base else spread * noise
        out[name] = jnp.asarray(drawn.astype(out[name].dtype))
    for name, factor in factors.items():
        out[name] = (out[name] * factor).astype(out[name].dtype)
    return out
```

```python
import concourse.bass as bass
from concourse import mybir
from contextlib import ExitStack

F32 = mybir.dt.float32
F16 = mybir.dt.float16
I32 = mybir.dt.int32
ALU = mybir.AluOpType
ACT = mybir.ActivationFunctionType
AX_X = mybir.AxisListType.X

P = 128
N = 2500
D = 512
DK = D // P
NT = -(-N // P)
NPAD = NT * P
LAST = N - (NT - 1) * P
R = 8
NW = 2 * R + 1
E = 80000
EC = E // P
STEPS = 4
ITS = NT // STEPS
PC = 4
ECP = R * NT * PC
BC = ECP // 2
WIN = 340
LT = 17
LTD = 2 * WIN
LIT = LTD // LT
VROWS = R * NPAD
K_BINS = 8
FT = 28
BINS = [-1.5, -1.0, -0.5, 0.0, 0.5, 1.0, 1.5]
RND = 12582912.0
YS = 512.0
FAR = -20000.0
assert EC * P == E and STEPS * ITS == NT and ECP >= EC and LIT * LT == LTD and LIT == R * ITS
assert all(n * P + NT * (P - 1) < (WIN + 1) * P for n in (BC, EC - BC))
assert N + K_BINS * (P - 1) < (FT + 1) * P
CHUNK_A = 9
PER_STEP = [range(0, 4), range(4, 8), range(8, 12), range(12, 17)]


def build(nc, x, src, dst, etype, w_self, b_self, w_rel, b_rel, w_ffn, out):
    ctx = ExitStack()
    with ctx:
        def sb(name, shape, dt):
            return ctx.enter_context(nc.sbuf_tensor(name, shape, dt))

        def sem(name):
            return ctx.enter_context(nc.semaphore(name))

        table = [nc.dram_tensor(f"table{d}", (VROWS, 2 * D), F16) for d in range(2)]
        rows = nc.dram_tensor("ffn_rows", (NPAD, 2 * D), I32)

        big = sb("big", [P, 36864], F16)
        yT = big[:, 0:2 * DK * NPAD].rearrange("p (h k n) -> p h k n", h=2, k=DK)
        wmov = big[:, 20480:28672].rearrange("p (b h k n) -> p b h k n", b=2, h=2, k=DK)
        wraw = [big[:, 20480 + 4096 * s:20480 + 4096 * (s + 1)].bitcast(F32) for s in range(4)]
        wf = big[:, 0:32768]
        wfraw = wraw[3]
        acc = sb("acc", [P, NT * D], F32)
        gath = sb("gath", [P, LT * 2 * D], F16)
        gf = gath[:, :].bitcast(F32)
        ytmp = gf[:, 0:4 * D].rearrange("p (s n) -> p s n", s=4)
        e0 = 4 * D
        ea = [gf[:, e0 + ECP * i:e0 + ECP * (i + 1)] for i in range(9)]
        e_src, e_dst, e_type = (a.bitcast(I32) for a in ea[0:3])
        e_bin, e_pos = ea[3], ea[4]
        e_tmp = [gf[:, ECP * i:ECP * (i + 1)].bitcast(I32) for i in range(2)]
        b0 = e0 + 9 * ECP
        braw = gf[0:64, b0:b0 + D]
        bh = gath[0:64, 2 * (b0 + D):2 * (b0 + D) + D]
        frow = gath[:, 0:4 * 4 * D].rearrange("p (s n) -> p s n", s=4)
        fyT = gath[:, 8192:8192 + 2 * 2 * D].rearrange("p (s n) -> p s n", s=2)
        fout = gath[:, 10240:10240 + 4096].bitcast(F32).rearrange("p (s n) -> p s n", s=4)
        xin = gath[:, 8192:12288].bitcast(F32).rearrange("p (s n) -> p s n", s=4)
        ftmp = gath[:, 12288:16384].bitcast(F32).rearrange("p (s n) -> p s n", s=4)

        trow = sb("trow", [P, 4, 2 * D], F16)
        wstage = sb("wstage", [P, DK, P], F32)
        bmov = sb("bmov", [P, D], F16)
        sel = sb("sel", [P, NW, P], F16)
        d2 = [sb(f"d2_{i}", [P, ECP], F16) for i in range(4)]
        e_row, e_col = [ea[5], d2[0][:, :]], [ea[6], d2[1][:, :]]
        e_hi, e_lo = [ea[7], d2[2][:, :]], [ea[8], d2[3][:, :]]
        work = sb("work", [P, 2, WIN], F32)
        ind, scan, dec = work[:, 0, 0:BC], work[:, 1, 0:BC], work
        zeros = sb("zeros", [P, BC], F16)
        ohc = sb("ohc", [P, 2 * PC, WIN], F16)
        ohr = sb("ohr", [P, 2 * PC, 2, P], F16)
        loc = sb("loc", [P, 2 * LTD], F16)
        gidx = sb("gidx", [P, 2 * LTD], I32)
        gidr = sb("gidr", [P, LT], I32)
        oh = sb("oh", [P, LT, P], F16)
        lbin = sb("lbin", [1, 2 * LTD], I32)
        iota_i = sb("iota_i", [P, WIN], I32)
        ge = iota_i[0:32, :].bitcast(F32)
        iota_f = sb("iota_f", [P, WIN], F32)
        iota_h = sb("iota_h", [P, WIN], F16)
        dif = sb("dif", [P, P], I32)
        difw = sb("difw", [P, NW], I32)
        selw = sb("selw", [P, 2, NW], F32)
        ident = sb("ident", [P, P], F32)
        ident_h = sb("ident_h", [P, P], F16)
        before = sb("before", [P, P], F32)
        ones = sb("ones", [P, P], F32)
        node1 = sb("node1", [P, NT], I32)
        node1f = sb("node1f", [P, NT], F32)
        invalid = sb("invalid", [P, NT], F32)
        ssq = sb("ssq", [P, NW + 1], F32)
        ssum = sb("ssum", [P, 1], F32)
        ex = sb("ex", [P, 12], I32)
        exf = sb("exf", [P, 12, K_BINS], I32)
        ssf = sb("ssf", [P, K_BINS], F32)
        st = sb("st", [P, NT, 6], F32)
        mv = sb("mv", [P, NT, 2], F32)
        ln = sb("ln", [P, 6, NT], F32)
        cnt = sb("cnt", [P, 2 * NT], F32)
        pre = sb("pre", [P, 2 * NT], F32)
        off = sb("off", [P, 2 * NT], F32)
        tcol = sb("tcol", [32, 4], F32)
        tbc = sb("tbc", [32, P], F32)
        fb = sb("fb", [P, 8, NT], F32)
        fd = sb("fd", [P, 4, FT], F32)
        fgi = sb("fgi", [P, FT], I32)
        fsi = sb("fsi", [P, FT], I32)
        fbin = sb("fbin", [1, FT], I32)
        ohrf = ohr[:, :, :, :].rearrange("p s h n -> p (s h n)").bitcast(F32)
        fsa = ohrf[:, 0:4 * P].rearrange("p (s n) -> p s n", s=4)
        fsc = ohrf[:, 4 * P:4 * (P + FT)].rearrange("p (s n) -> p s n", s=4)

        bank = [ctx.enter_context(nc.psum_tensor(f"bank{i}", [P, D], F32)) for i in range(8)]
        pj = bank[0:2]
        wt = bank[2]
        pm = bank[3:5]
        ag = bank[5:8]

        ld_x = [sem(f"ld_x{i}") for i in range(ITS)]
        ld_edges = sem("ld_edges")
        ld_b = sem("ld_b")
        ld_sq = [sem(f"ld_sq{i}") for i in range(4)]
        ld_wc = sem("ld_wc")
        ld_wf = sem("ld_wf")
        ld_x2 = [sem(f"ld_x2{i}") for i in range(4)]
        consts_i = sem("consts_i")
        consts = sem("consts")
        pads = sem("pads")
        squares = sem("squares")
        step = sem("step")
        root = sem("root")
        small_in = sem("small_in")
        small_out = sem("small_out")
        y_ready = sem("y_ready")
        yt_mm = sem("yt_mm")
        yt_hi = sem("yt_hi")
        yt_lo = sem("yt_lo")
        wt_mm = sem("wt_mm")
        wt_hi = sem("wt_hi")
        wt_lo = sem("wt_lo")
        proj = sem("proj")
        proj_hi = sem("proj_hi")
        proj_read = sem("proj_read")
        row_out = [sem(f"row_out{i}") for i in range(4)]
        rank = sem("rank")
        code_ready = sem("code_ready")
        code_used = sem("code_used")
        perm_done = sem("perm_done")
        lists = sem("lists")
        oh_ready = sem("oh_ready")
        agg = sem("agg")
        agg_read = sem("agg_read")
        got = [sem(f"got{i}") for i in range(LT)]
        idx_copied = sem("idx_copied")
        wf_sq = sem("wf_sq")
        wf_hi = sem("wf_hi")
        wf_lo = sem("wf_lo")
        x1_done = sem("x1_done")
        f_y = sem("f_y")
        f_hi = sem("f_hi")
        f_lo = sem("f_lo")
        f_rows = [sem(f"f_rows{i}") for i in range(4)]
        f_x1 = sem("f_x1")
        f_code = sem("f_code")
        f_used = sem("f_used")
        f_perm = sem("f_perm")
        f_idx = sem("f_idx")
        f_got = [sem(f"f_got{i}") for i in range(4)]
        f_tr = sem("f_tr")
        f_yT = sem("f_yT")
        f_mm = sem("f_mm")
        f_add = sem("f_add")
        f_out = [sem(f"f_out{i}") for i in range(4)]

        block = ctx.enter_context(nc.Block())
        w_order = list(range(1, NW)) + [0]

        def w_dram(w):
            return w_self if w == 0 else w_rel[w - 1]

        @block.sync
        def _(sp):
            xg = x[0:(NT - 1) * P, :].rearrange("(t p) d -> p t d", p=P)
            accv = acc[:, :].rearrange("p (t d) -> p t d", t=NT)
            for g in range(ITS):
                hi = min(STEPS * (g + 1), NT - 1)
                sp.dma_start(accv[:, STEPS * g:hi, :], xg[:, STEPS * g:hi, :]).then_inc(ld_x[g], 16)
            sp.wait_ge(pads, 1)
            sp.dma_start(accv[0:LAST, NT - 1, :], x[(NT - 1) * P:N, :]).then_inc(ld_x[ITS - 1], 16)
            for i, w in enumerate(w_order):
                if i >= 4:
                    sp.wait_ge(squares, i - 3)
                sp.dma_start(wraw[(i + 2) % 4].rearrange("p (c d) -> p c d", c=DK),
                             w_dram(w).rearrange("(c p) d -> p c d", p=P)).then_inc(ld_sq[(i + 2) % 4], 16)
                if i == 3:
                    sp.wait_ge(pads, 3)
                    for row in (0, 32):
                        sp.dma_start(braw[row:row + 1, :], b_self.rearrange("(a d) -> a d", a=1)).then_inc(ld_b, 16)
                        sp.dma_start(braw[row + 1:row + NW, :], b_rel).then_inc(ld_b, 16)
                    for tile, edges in ((e_src, src), (e_dst, dst), (e_type, etype)):
                        sp.dma_start(tile[:, 0:EC], edges.rearrange("(p f) -> p f", p=P)).then_inc(ld_edges, 16)

            def w_chunk(w, q):
                sp.wait_ge(wt_mm, 4 * w + q + 4)
                sp.dma_start(wstage[:, :, :],
                             w_rel[bass.ds(w, 1), :, bass.ds(q * P, P)].rearrange("a (c p) d -> p (a c) d", p=P)).then_inc(ld_wc, 16)

            def store_rows(w, q, u, d, r):
                sp.wait_ge(proj_read, NT * w + STEPS * q + u + 3)
                sp.dma_start(table[d].ap()[bass.ds((r * NT + STEPS * q + u) * P, P), :],
                             trow[:, u, :]).then_inc(row_out[u], 16)

            with sp.Fori(0, DK) as q:
                w_chunk(0, q)

            def relation(w, d, r, chunks=True):
                with sp.Fori(0, DK) as q:
                    if chunks:
                        w_chunk(w, q)
                    for u in range(STEPS):
                        store_rows(w, q, u, d, r)
                for u in range(STEPS):
                    store_rows(w, DK, u, d, r)

            with sp.Fori(0, 4) as pair:
                for par in range(2):
                    relation(2 * pair + par + 1, 0, 2 * pair + par)
            with sp.Fori(0, 3) as pair:
                for par in range(2):
                    relation(2 * pair + par + 9, 1, 2 * pair + par)
            relation(15, 1, 6)
            relation(16, 1, 7, chunks=False)

            for k in range(K_BINS):
                if k == 0:
                    sp.wait_ge(proj_read, NT * NW + 2)
                else:
                    sp.wait_ge(wf_lo, k)
                sp.dma_start(wfraw.rearrange("p (c o) -> p c o", c=DK),
                             w_ffn[k].rearrange("(c p) o -> p c o", p=P)).then_inc(ld_wf, 16)

            sp.wait_ge(agg, 2 * LTD + LT)

            def load_x(j, u, n=P):
                sp.dma_start(xin[0:n, u, :], x[bass.ds(j * P, n), :]).then_inc(ld_x2[u], 16)

            for u in range(STEPS):
                load_x(u, u)
            with sp.Fori(1, ITS - 1) as i:
                for u in range(STEPS):
                    sp.wait_ge(x1_done, STEPS * i + u - STEPS + 1)
                    load_x(STEPS * i + u, u)
            for u in range(STEPS):
                j = NT - STEPS + u
                sp.wait_ge(x1_done, j - STEPS + 1)
                load_x(j, u, P if j < NT - 1 else LAST)

            with sp.Fori(0, ITS) as i:
                for u in range(STEPS):
                    j = STEPS * i + u
                    sp.wait_ge(f_lo, j + 1)
                    sp.dma_start(rows.ap()[bass.ds(j * P, P), 0:D], trow[:, u, :].bitcast(I32)).then_inc(f_rows[u], 16)
                    sp.dma_start(rows.ap()[bass.ds(j * P, P), D:2 * D],
                                 acc[:, bass.ds(j * D, D)].bitcast(I32)).then_inc(f_x1, 16)

        @block.gpsimd
        def _(pool):
            nc.gpsimd.iota(iota_i[:, :], pattern=[[1, WIN]], base=0, channel_multiplier=0)
            nc.gpsimd.iota(dif[:, :], pattern=[[1, P]], base=0, channel_multiplier=-1)
            nc.gpsimd.iota(difw[:, :], pattern=[[1, NW]], base=0, channel_multiplier=-1)
            nc.gpsimd.iota(node1[:, :], pattern=[[P, NT]], base=1, channel_multiplier=1).then_inc(consts_i, 1)

            def gather_set(i, d, which):
                v0, v1 = (0, CHUNK_A) if which == 0 else (CHUNK_A, LT)
                pool.wait_ge(agg, LT * i + v1)
                nc.gpsimd.tensor_copy(gidr[:, v0:v1], gidx[:, bass.ds(LT * i + v0, v1 - v0)]).then_inc(idx_copied, 1)
                pool.wait_ge(idx_copied, 2 * i + which + 1)
                pool.nop(nofuse=True)
                for v in range(v0, v1):
                    pool.indirect_dma_start(
                        out=gath[:, v * 2 * D:(v + 1) * 2 * D], out_offset=None, in_=table[d].ap(),
                        in_offset=bass.IndirectOffsetOnAxis(ap=gidr[:, v:v + 1], axis=0)).then_inc(got[v], 16)

            for d in range(2):
                pool.wait_ge(lists, 2 * d + 2)
                for u in range(4):
                    pool.wait_ge(row_out[u], 16 * (1 + R * ITS * (d + 1)))
                with pool.Fori(LIT * d, LIT * (d + 1)) as i:
                    for which in range(2):
                        gather_set(i, d, which)

            pool.wait_ge(f_idx, 1)
            for u in range(4):
                pool.wait_ge(f_rows[u], 16 * ITS)
            pool.wait_ge(f_x1, 16 * NT)

            def fetch(t):
                pool.indirect_dma_start(out=frow[:, t % 4, :].bitcast(I32), out_offset=None, in_=rows.ap(),
                                        in_offset=bass.IndirectOffsetOnAxis(ap=fgi[:, t:t + 1], axis=0)
                                        ).then_inc(f_got[t % 4], 16)

            def send(t):
                pool.wait_ge(f_add, t + 3)
                pool.indirect_dma_start(out=out, out_offset=bass.IndirectOffsetOnAxis(ap=fsi[:, t:t + 1], axis=0),
                                        in_=fout[:, t % 4, :], in_offset=None,
                                        bounds_check=N - 1, oob_is_err=False).then_inc(f_out[t % 4], 16)

            for t in range(4):
                fetch(t)
            for t in range(FT):
                send(t)
                if t + 4 < FT:
                    fetch(t + 4)
            for u in range(4):
                pool.wait_ge(f_out[u], 16 * (FT // 4))

        @block.scalar
        def _(act):
            nc.scalar.sem_inc(agg_read, 2)
            nc.scalar.sem_inc(f_yT, 2)
            for i, w in enumerate(w_order):
                act.wait_ge(ld_sq[(i + 2) % 4], 16 * (i // 4 + 1))
                if i == 0:
                    act.wait_ge(pads, 2)
                if i:
                    act.wait_ge(squares, i)
                nc.scalar.activation(trow[:, 0:2, :].rearrange("p s n -> p (s n)"), wraw[(i + 2) % 4], ACT.Square,
                                     accum_out=ssq[:, w:w + 1]).then_inc(squares, 1)
            act.wait_ge(ld_b, 64)
            nc.scalar.activation(trow[0:NW, 2, 0:D], braw[0:NW, :], ACT.Square, scale=1.0 / 32,
                                 accum_out=ssq[0:NW, NW:NW + 1]).then_inc(squares, 1)

            act.wait_ge(root, 1)
            nc.scalar.activation(ln[:, 1, :], ln[:, 0, :], ACT.Sqrt).then_inc(root, 1)
            with act.Fori(0, NT // 2) as i:
                for u in range(2):
                    act.wait_ge(yt_mm, 2 * i + u + 1)
                    nc.scalar.copy(yT[:, 0, :, bass.ds((2 * i + u) * P, P)],
                                   pj[u][:, :].rearrange("p (k n) -> p k n", k=DK)).then_inc(yt_hi, 1)

            def w_high(buf, c, q):
                act.wait_ge(wt_mm, c + 1)
                nc.scalar.activation(wmov[:, buf, 0, q, :] if isinstance(q, int) else
                                     wmov[:, buf, 0].rearrange("p k n -> p (k n)")[:, bass.ds(q * D, D)],
                                     wt[:, :], ACT.Copy, scale=ex[:, 3:4].bitcast(F32)).then_inc(wt_hi, 1)

            act.wait_ge(small_in, 7)
            for q in range(DK):
                w_high(0, q, q)
            with act.Fori(0, DK) as q:
                w_high(1, 4 + q, q)

            act.wait_ge(squares, NW + 1)

            def row_high(w, q, u):
                act.wait_ge(proj, NT * w + STEPS * q + u + 1)
                act.wait_ge(row_out[u], 16 * (ITS * (w - 1) + q + 1))
                nc.scalar.activation(trow[:, u, 0:D], pj[u % 2][:, :], ACT.Copy,
                                     scale=2.0 ** -14).then_inc(proj_hi, 1)

            def relation(w, nxt, chunks=True):
                with act.Fori(0, DK) as q:
                    for u in range(STEPS):
                        row_high(w, q, u)
                        if u == 2 and chunks:
                            w_high(nxt, 4 * (w + 1) + q, q)
                for u in range(STEPS):
                    row_high(w, DK, u)

            with act.Fori(0, 7) as pair:
                for par in range(2):
                    relation(2 * pair + par + 1, par)
            relation(15, 0)
            relation(16, 1, chunks=False)

            for u in range(4):
                act.wait_ge(row_out[u], 16 * (1 + 2 * R * ITS))
            for k in range(K_BINS):
                act.wait_ge(ld_wf, 16 * (k + 1))
                if k:
                    act.wait_ge(wf_sq, k)
                nc.scalar.activation(trow[:, 0:2, :].rearrange("p s n -> p (s n)"), wfraw, ACT.Square,
                                     accum_out=ssf[:, k:k + 1]).then_inc(wf_sq, 1)
                act.wait_ge(small_in, 13 + k)
                nc.scalar.activation(wf[:, 4096 * k:4096 * k + 2048], wfraw, ACT.Copy,
                                     scale=exf[:, 3, k:k + 1].bitcast(F32)).then_inc(wf_hi, 1)

            act.wait_ge(wf_sq, K_BINS)
            act.wait_ge(root, 3)
            nc.scalar.activation(ln[:, 1, :], ln[:, 0, :], ACT.Sqrt).then_inc(root, 1)
            for u in range(STEPS):
                act.wait_ge(f_y, u + 1)
                nc.scalar.copy(trow[:, u, 0:D], ftmp[:, u, :]).then_inc(f_hi, 1)
            with act.Fori(1, ITS) as i:
                for u in range(STEPS):
                    act.wait_ge(f_y, STEPS * i + u + 1)
                    act.wait_ge(f_rows[u], 16 * i)
                    nc.scalar.copy(trow[:, u, 0:D], ftmp[:, u, :]).then_inc(f_hi, 1)

            with act.Fori(0, FT // 4) as i:
                for u in range(4):
                    act.wait_ge(f_tr, 4 * i + u + 1)
                    nc.scalar.copy(fyT[:, u % 2, :], pj[u % 2][:, :].bitcast(F16)).then_inc(f_yT, 1)

        @block.tensor
        def _(pe):
            nc.tensor.sem_inc(code_used, 2)
            nc.tensor.sem_inc(agg, LT)

            pe.wait_ge(consts, 1)
            with pe.Fori(0, NT // 4) as i:
                for u in range(4):
                    pe.wait_ge(y_ready, 4 * i + u + 1)
                    pe.wait_ge(yt_lo, 4 * i + u + 1)
                    for k in range(DK):
                        mm = nc.tensor.transpose(pj[u % 2][:, k * P:(k + 1) * P], ytmp[:, u, k * P:(k + 1) * P],
                                                 ident[:, :])
                    mm.then_inc(yt_mm, 1)

            def small(outp, lhsT, rhs):
                return nc.tensor.matmul(outp, lhsT, rhs, start=True, stop=True)


            def offsets(base, n_bins=NT, blocks=2, win=WIN):
                pe.wait_ge(small_in, base)
                small(ag[0][:, 0:blocks * n_bins], before[:, :], cnt[:, 0:blocks * n_bins])
                for b in range(blocks):
                    mm = small(ag[1][0:n_bins, b:b + 1], cnt[:, b * n_bins:(b + 1) * n_bins], ones[:, 0:1])
                mm.then_inc(small_out, 1)
                for b in range(blocks):
                    pe.wait_ge(small_in, base + 1 + 2 * b)
                    small(ag[0][:, 0:n_bins], tbc[0:n_bins, :], before[0:n_bins, 0:n_bins])
                    small(ag[1][0:n_bins, 0:1], before[0:n_bins, 0:n_bins], tcol[0:n_bins, b:b + 1]
                          ).then_inc(small_out, 1)
                    pe.wait_ge(small_in, base + 2 + 2 * b)
                    small(ag[2][0:1, 0:win], ones[0:n_bins, 0:1], ge[0:n_bins, 0:win]).then_inc(small_out, 1)

            offsets(1)

            pe.wait_ge(small_in, 6)
            small(ag[0][:, 0:1], ones[:, :], ssum[:, :]).then_inc(small_out, 1)

            def w_transpose(c, raw):
                pe.wait_ge(wt_lo, c + 1)
                for oc in range(DK):
                    mm = nc.tensor.transpose(wt[:, oc * P:(oc + 1) * P], raw[oc], ident[:, :])
                mm.then_inc(wt_mm, 1)

            pe.wait_ge(ld_sq[(NW - 1 + 2) % 4], 16 * ((NW - 1) // 4 + 1))
            self_raw = wraw[(NW - 1 + 2) % 4]
            for q in range(DK):
                w_transpose(q, [self_raw[:, oc * D + q * P:oc * D + (q + 1) * P] for oc in range(DK)])
            stage = [wstage[:, oc, :] for oc in range(DK)]

            def project(w, buf, q, u):
                j = STEPS * q + u
                pe.wait_ge(proj_read, NT * w + j + 1)
                pe.nop(nofuse=True)
                ps = pj[u % 2][:, :]
                nc.tensor.matmul(ps, sel[:, :, :].rearrange("p w n -> p (w n)")[:, bass.ds(w * P, P)], bmov[:, :],
                                 start=True, stop=False)
                for k in range(DK):
                    yh = big[:, bass.ds(k * NPAD + j * P, P)]
                    yl = big[:, bass.ds((DK + k) * NPAD + j * P, P)]
                    nc.tensor.matmul(ps, yh, wmov[:, buf, 0, k, :], start=False, stop=False)
                    nc.tensor.matmul(ps, yh, wmov[:, buf, 1, k, :], start=False, stop=False)
                    mm = nc.tensor.matmul(ps, yl, wmov[:, buf, 0, k, :], start=False, stop=(k == DK - 1))
                mm.then_inc(proj, 1)

            pe.wait_ge(yt_lo, NT + 2)
            pe.wait_ge(wt_lo, DK + 1)
            with pe.Fori(0, DK) as q:
                for u in range(STEPS):
                    project(0, 0, q, u)
                    if u == 2:
                        pe.wait_ge(ld_wc, 16 * (q + 1))
                        w_transpose(4 + q, stage)
            for u in range(STEPS):
                project(0, 0, DK, u)

            def permute(w, q, u):
                pe.wait_ge(code_ready, NT * (w - 1) + STEPS * q + u + 1)
                for v in range(PC):
                    s = (u % 2) * PC + v
                    for h in range(2):
                        mm = nc.tensor.matmul(pm[h][:, 0:WIN], ohr[:, s, h, :], ohc[:, s, :], start=False, stop=False,
                                              skip_group_check=True)
                mm.then_inc(code_used, 1)

            def open_block(b):
                if b:
                    pe.wait_ge(lists, b)
                for h in range(2):
                    nc.tensor.matmul(pm[h][:, 0:WIN], zeros[:, 0:P], iota_h[:, :], start=True,
                                     stop=False, skip_group_check=True)

            def close_block():
                for h in range(2):
                    mm = nc.tensor.matmul(pm[h][:, 0:WIN], zeros[:, 0:P], iota_h[:, :], start=False,
                                          stop=True, skip_group_check=True)
                mm.then_inc(perm_done, 1)

            def sum_tile(i, v):
                t = LT * i + v
                pe.wait_ge(oh_ready, t + 1)
                pe.wait_ge(got[v], 16 * (i + 1))
                pe.wait_ge(agg_read, t if v >= 2 else t + 1)
                nc.tensor.matmul(ag[v % 3][:, :], oh[:, v, :], gath[:, v * 2 * D:v * 2 * D + D], start=True, stop=False)
                nc.tensor.matmul(ag[v % 3][:, :], oh[:, v, :], gath[:, v * 2 * D + D:(v + 1) * 2 * D], start=False,
                                 stop=True).then_inc(agg, 1)

            def iteration(w, buf, q, chunk, summing):
                for u in range(STEPS):
                    project(w, buf, q, u)
                    if u == 2 and chunk:
                        pe.wait_ge(ld_wc, 16 * (4 * w + q + 1))
                        w_transpose(4 * (w + 1) + q, stage)
                    if summing:
                        for v in PER_STEP[u]:
                            sum_tile(ITS * (w - 1 - R) + q, v)
                    permute(w, q, u)

            def relation(w, par, summing, chunks=True):
                pe.wait_ge(wt_lo, 4 * (w + 1) + 1)
                pe.nop(nofuse=True)
                with pe.Fori(0, DK) as q:
                    iteration(w, 1 - par, q, chunks, summing)
                iteration(w, 1 - par, DK, False, summing)

            open_block(0)
            for rp in range(2):
                for par in range(2):
                    relation(2 * rp + par + 1, par, False)
                if rp == 0:
                    offsets(8)
            close_block()
            open_block(1)
            with pe.Fori(2, 4) as rp:
                for par in range(2):
                    relation(2 * rp + par + 1, par, False)
            close_block()
            open_block(2)
            with pe.Fori(4, 6) as rp:
                for par in range(2):
                    relation(2 * rp + par + 1, par, True)
            close_block()
            open_block(3)
            for par in range(2):
                relation(12 + par + 1, par, True)
            relation(15, 0, True)
            relation(16, 1, True, chunks=False)
            close_block()

            with pe.Fori(0, K_BINS) as k:
                with pe.Fori(0, ITS) as q:
                    for v in range(LT):
                        sum_tile(LIT + ITS * k + q, v)
                pe.wait_ge(wf_sq, k + 1)
                pe.wait_ge(small_in, 12 + k)
                small(pj[0][:, 0:K_BINS], ones[:, :], ssf[:, :]).then_inc(small_out, 1)

            offsets(21, K_BINS, 1, FT)
            for n in range(NT):
                pe.wait_ge(f_code, n + 1)
                nc.tensor.matmul(pm[0][:, 0:FT], fsa[:, n % 4, :], fsc[:, n % 4, :], start=(n == 0),
                                 stop=(n == NT - 1)).then_inc(f_used, 1)

            def f_transpose(m, slot, uses):
                pe.wait_ge(f_got[slot], 16 * uses)
                pe.wait_ge(f_yT, m + 1)
                for c in range(2 * DK):
                    mm = nc.tensor.transpose(pj[slot % 2][:, :].bitcast(F16)[:, c * P:(c + 1) * P],
                                             frow[:, slot, c * P:(c + 1) * P], ident_h[:, :])
                mm.then_inc(f_tr, 1)

            def f_product(t, slot):
                pe.wait_ge(f_yT, t + 3)
                pe.wait_ge(f_add, t + 1)
                pe.nop(nofuse=True)
                kb = pe.value_load(fbin[0:1, bass.ds(t, 1)], min_val=0, max_val=K_BINS - 1)
                ps = ag[slot % 2][:, :]
                for k in range(DK):
                    wh = wf[:, bass.ds(kb * 4096 + k * D, D)]
                    wl = wf[:, bass.ds(kb * 4096 + 2048 + k * D, D)]
                    yh = fyT[:, slot % 2, k * P:(k + 1) * P]
                    yl = fyT[:, slot % 2, (DK + k) * P:(DK + k + 1) * P]
                    nc.tensor.matmul(ps, yh, wh, start=(k == 0), stop=False)
                    nc.tensor.matmul(ps, yh, wl, start=False, stop=False)
                    mm = nc.tensor.matmul(ps, yl, wh, start=False, stop=(k == DK - 1))
                mm.then_inc(f_mm, 1)

            pe.wait_ge(wf_lo, K_BINS)
            pe.wait_ge(f_idx, 1)
            f_transpose(0, 0, 1)
            with pe.Fori(0, FT // 4 - 1) as i:
                for u in range(4):
                    f_transpose(4 * i + u + 1, (u + 1) % 4, i + 1 + (u == 3))
                    f_product(4 * i + u, u)
            for u in range(4):
                t = FT - 4 + u
                if u < 3:
                    f_transpose(t + 1, u + 1, FT // 4)
                f_product(t, u)

        @block.vector
        def _(dve):
            V = nc.vector
            V.sem_inc(yt_lo, 2)
            V.sem_inc(wt_lo, 1)
            V.sem_inc(proj_read, 2)
            V.sem_inc(f_add, 2)
            for u in range(4):
                V.sem_inc(row_out[u], 16)
            steps = [0]

            def chain(ins):
                steps[0] += 1
                ins.then_inc(step, 1)
                dve.wait_ge(step, steps[0])

            V.memset(acc[:, (NT - 1) * D:NT * D], 0.0).then_inc(pads, 1)
            V.memset(ssq[:, :], 0.0).then_inc(pads, 1)
            V.memset(braw, 0.0)
            V.memset(e_src[:, EC:ECP], NPAD)
            V.memset(e_dst[:, EC:ECP], NPAD)
            V.memset(e_type[:, EC:ECP], 0).then_inc(pads, 1)

            V.memset(ones[:, :], 1.0)
            V.memset(zeros[:, :], 0.0)
            V.memset(bmov[:, :], 0.0)
            chain(V.memset(ssf[:, :], 0.0))
            dve.wait_ge(consts_i, 1)
            V.tensor_copy(iota_f[:, :], iota_i[:, :])
            V.tensor_copy(iota_h[:, :], iota_i[:, :])
            V.tensor_scalar(ident_h[:, :], dif[:, :], 0.0, None, ALU.is_equal)
            V.tensor_scalar(before[:, :], dif[:, :], 0.0, None, ALU.is_gt)
            V.tensor_copy(node1f[:, :], node1[:, :])
            V.tensor_scalar(invalid[:, :], node1[:, :], float(N), -100.0, ALU.is_gt, ALU.mult)
            V.tensor_scalar(selw[:, 0, :], difw[:, :], 0.0, 2.0 ** 13, ALU.is_equal, ALU.mult)
            V.tensor_scalar(selw[:, 1, :], difw[:, :], -32.0, 2.0 ** 13, ALU.is_equal, ALU.mult)
            V.tensor_scalar(ident[:, :], dif[:, :], 0.0, None, ALU.is_equal).then_inc(consts, 1)
            dve.wait_ge(consts, 1)
            chain(V.tensor_tensor(selw[:, 0, :], selw[:, 0, :], selw[:, 1, :], ALU.add))
            for w in range(NW):
                last = V.tensor_scalar(sel[:, w, :], ones[:, :], selw[:, 0, w:w + 1], None, ALU.mult)
            chain(last)

            def norm_factors(at):
                V.tensor_scalar(ln[:, 0, :], mv[:, :, 1], 1e-5, None, ALU.add).then_inc(root, 1)
                dve.wait_ge(root, at + 2)
                chain(V.reciprocal(ln[:, 2, :], ln[:, 1, :]))
                chain(V.tensor_tensor(ln[:, 3, :], ln[:, 0, :], ln[:, 2, :], ALU.mult))
                chain(V.tensor_tensor(ln[:, 2, :], ln[:, 1, :], ln[:, 3, :], ALU.add))
                chain(V.tensor_scalar(ln[:, 3, :], ln[:, 2, :], 0.5, None, ALU.mult))
                chain(V.reciprocal(ln[:, 2, :], ln[:, 3, :]))
                V.tensor_scalar(ln[:, 5, :], ln[:, 2, :], YS, None, ALU.mult)
                chain(V.tensor_scalar(ln[:, 4, :], mv[:, :, 0], -1.0, None, ALU.mult))

            for g in range(ITS):
                dve.wait_ge(ld_x[g], 32 if g == ITS - 1 else 16)
                for j in range(STEPS * g, STEPS * (g + 1)):
                    last = V.bn_stats(st[:, j, :], acc[:, j * D:(j + 1) * D])
            chain(last)
            for j in range(NT):
                last = V.bn_aggr(mv[:, j, :], st[:, j, :])
            chain(last)
            norm_factors(0)

            def normed(n, u, tile, done):
                V.tensor_scalar(tile[:, u, :], acc[:, bass.ds(n * D, D)], ln[:, 4, bass.ds(n, 1)],
                                ln[:, 5, bass.ds(n, 1)], ALU.add, ALU.mult).then_inc(done, 1)

            def y_low(n, u):
                dve.wait_ge(yt_hi, n + 1)
                V.tensor_tensor(yT[:, 1, :, bass.ds(n * P, P)], pj[u % 2][:, :].rearrange("p (k n) -> p k n", k=DK),
                                yT[:, 0, :, bass.ds(n * P, P)], ALU.subtract).then_inc(yt_lo, 1)

            for n in range(2):
                normed(n, n, ytmp, y_ready)
            with dve.Fori(0, ITS - 1) as i:
                for u in range(STEPS):
                    normed(STEPS * i + u + 2, (u + 2) % 4, ytmp, y_ready)
                    y_low(STEPS * i + u, u)
            for u in range(STEPS):
                if u < 2:
                    normed(NT - STEPS + u + 2, u + 2, ytmp, y_ready)
                y_low(NT - STEPS + u, u)

            dve.wait_ge(ld_edges, 48)

            def prepare(d):
                node, other = (e_src, e_dst) if d == 0 else (e_dst, e_src)
                a, b = e_tmp
                chain(V.tensor_scalar(a, node, 7, None, ALU.logical_shift_right))
                chain(V.tensor_copy(e_bin, a))
                chain(V.scalar_tensor_tensor(out=a, in0=e_type, scalar=float(NPAD), in1=other, op0=ALU.mult,
                                             op1=ALU.add))
                chain(V.tensor_scalar(b, a, 11, None, ALU.logical_shift_right))
                chain(V.tensor_scalar(e_pos.bitcast(I32), a, 2047, None, ALU.bitwise_and))
                chain(V.tensor_copy(e_lo[d][:, :], e_pos.bitcast(I32)))
                chain(V.tensor_scalar(a, node, P - 1, None, ALU.bitwise_and))
                chain(V.scalar_tensor_tensor(out=e_hi[d][:, :], in0=a, scalar=float(VROWS // 2048), in1=b, op0=ALU.mult,
                                             op1=ALU.add))
                chain(V.tensor_scalar(e_hi[d][:, :], e_hi[d][:, :], 1.0, None, ALU.add))
                chain(V.memset(e_pos, FAR))

            def count_bin(m, blk, b):
                V.tensor_scalar((ind, scan)[blk], e_bin[:, blk * BC:(blk + 1) * BC], iota_f[:, bass.ds(b, 1)], None,
                                ALU.is_equal, ALU.add, accum_out=cnt[:, bass.ds(blk * NT + b, 1)]).then_inc(rank, 1)
                dve.wait_ge(rank, m + 1)

            def rank_bin(m, blk, b):
                cols = slice(blk * BC, (blk + 1) * BC)
                V.tensor_scalar(ind, e_bin[:, cols], iota_f[:, bass.ds(b, 1)], None,
                                ALU.is_equal).then_inc(rank, 1)
                dve.wait_ge(rank, m + 1)
                V.tensor_tensor_scan(scan, ind, zeros[:, :], off[:, bass.ds(blk * NT + b, 1)], ALU.add,
                                     ALU.add).then_inc(rank, 1)
                dve.wait_ge(rank, m + 2)
                dve.nop(nofuse=True)
                V.copy_predicated(e_pos[:, cols], ind.bitcast(I32), scan).then_inc(rank, 1)
                dve.wait_ge(rank, m + 3)

            def round_up_tiles(n_bins, blocks):
                t = tcol[0:n_bins, 0:blocks]
                chain(V.tensor_scalar(t, ag[1][0:n_bins, 0:blocks], 63.5, 1.0 / P, ALU.add, ALU.mult))
                chain(V.tensor_scalar(t, t, RND, None, ALU.add))
                chain(V.tensor_scalar(t, t, -RND, None, ALU.add))

            def offsets(out0, bins_out, n_bins=NT, blocks=2, win=WIN):
                dve.wait_ge(small_out, out0 + 1)
                chain(V.tensor_scalar(pre[:, 0:blocks * n_bins], ag[0][:, 0:blocks * n_bins], -1.0, None, ALU.add))
                round_up_tiles(n_bins, blocks)
                for b in range(blocks):
                    cols = slice(b * n_bins, (b + 1) * n_bins)
                    V.tensor_scalar(tbc[0:n_bins, :], ones[0:n_bins, :], tcol[0:n_bins, b:b + 1], None,
                                    ALU.mult).then_inc(small_in, 1)
                    dve.wait_ge(small_out, out0 + 2 + 2 * b)
                    chain(V.scalar_tensor_tensor(out=off[:, cols], in0=ag[0][:, 0:n_bins], scalar=float(P),
                                                 in1=pre[:, cols], op0=ALU.mult, op1=ALU.add))
                    V.tensor_scalar(ge[0:n_bins, 0:win], iota_f[0:n_bins, 0:win], ag[1][0:n_bins, 0:1], None,
                                    ALU.is_ge).then_inc(small_in, 1)
                    dve.wait_ge(small_out, out0 + 3 + 2 * b)
                    chain(V.tensor_scalar(bins_out[:, b * win:(b + 1) * win], ag[2][0:1, 0:win], -1.0, None,
                                          ALU.add))

            def slot_places(pos, col, row, tmp=None):
                tmp = e_tmp[0].bitcast(F32)[:, 0:pos.shape[1]] if tmp is None else tmp
                chain(V.tensor_scalar(tmp, pos, -63.5, 1.0 / P, ALU.add, ALU.mult))
                chain(V.tensor_scalar(tmp, tmp, RND, None, ALU.add))
                chain(V.tensor_scalar(col, tmp, -RND, None, ALU.add))
                chain(V.scalar_tensor_tensor(out=row, in0=col, scalar=-float(P), in1=pos, op0=ALU.mult, op1=ALU.add))

            prepare(0)
            with dve.Fori(0, NT) as b:
                for blk in range(2):
                    count_bin(2 * b + blk, blk, b)
            dve.sem_inc(small_in, 1)
            offsets(0, lbin[:, 0:LTD])

            def scales(total, e, extra=False):
                f = [e(c) for c in range(12)]
                chain(V.tensor_scalar(f[0].bitcast(F32), total, 1e-30, None, ALU.add))
                chain(V.tensor_scalar(f[1], f[0], 23, None, ALU.logical_shift_right))
                chain(V.tensor_scalar(f[2], f[1], 1.0, None, ALU.add))
                chain(V.tensor_scalar(f[4], f[2], 1, None, ALU.logical_shift_right))
                V.tensor_scalar(f[5], f[4], -1.0, 204.0, ALU.mult, ALU.add)
                V.tensor_scalar(f[8], f[4], 55.0, None, ALU.add)
                V.tensor_scalar(f[10], f[4], -1.0, 200.0, ALU.mult, ALU.add)
                chain(V.tensor_scalar(f[6], f[4], 41.0, None, ALU.add))
                V.tensor_scalar(f[3], f[5], 23, None, ALU.logical_shift_left)
                V.tensor_scalar(f[9], f[8], 23, None, ALU.logical_shift_left)
                V.tensor_scalar(f[11], f[10], 23, None, ALU.logical_shift_left)
                return V.tensor_scalar(f[7], f[6], 23, None, ALU.logical_shift_left)

            dve.wait_ge(squares, NW + 1)
            V.tensor_reduce(ssum[:, :], ssq[:, :], AX_X, ALU.add).then_inc(small_in, 1)
            dve.wait_ge(small_out, 6)
            chain(scales(ag[0][:, 0:1], lambda c: ex[:, c:c + 1]))
            w_scale = ex[:, 3:4].bitcast(F32)
            self_scale = ex[:, 7:8].bitcast(F32)
            agg_scale = ex[:, 9:10].bitcast(F32)
            dve.wait_ge(ld_b, 64)
            chain(V.tensor_scalar(braw, braw, ex[0:64, 11:12].bitcast(F32), None, ALU.mult))
            chain(V.tensor_copy(bh, braw))
            V.tensor_copy(bmov[0:32, :], bh[0:32, :])
            V.tensor_tensor(bmov[32:64, :], braw[32:64, :], bh[32:64, :], ALU.subtract).then_inc(small_in, 1)

            def w_low(buf, c, q):
                dve.wait_ge(wt_hi, c + 1)
                V.scalar_tensor_tensor(
                    out=wmov[:, buf, 1].rearrange("p k n -> p (k n)")[:, bass.ds(q * D, D)], in0=wt[:, :],
                    scalar=w_scale, in1=wmov[:, buf, 0].rearrange("p k n -> p (k n)")[:, bass.ds(q * D, D)],
                    op0=ALU.mult, op1=ALU.subtract).then_inc(wt_lo, 1)

            for q in range(DK):
                w_low(0, q, q)

            def self_step(q, u):
                b = STEPS * q + u
                for blk in range(2):
                    rank_bin(2 * NT + 6 * b + 3 * blk, blk, b)
                dve.wait_ge(proj, b + 1)
                V.tensor_scalar(acc[:, bass.ds(b * D, D)], pj[u % 2][:, :], self_scale, None,
                                ALU.mult).then_inc(proj_read, 1)

            with dve.Fori(0, DK) as q:
                for u in range(STEPS):
                    self_step(q, u)
                    if u == 2:
                        w_low(1, 4 + q, q)
            for u in range(STEPS):
                self_step(DK, u)
            slot_places(e_pos, e_col[0], e_row[0])
            prepare(1)

            def codes(w, q, u, d):
                ps = NT * (w - 1) + STEPS * q + u
                dve.wait_ge(code_used, ps + 1)
                for v in range(PC):
                    s = (u % 2) * PC + v
                    f = PC * (ps - d * R * NT) + v
                    V.tensor_scalar(ohc[:, s, :], iota_h[:, :], e_col[d][:, bass.ds(f, 1)], None, ALU.is_equal)
                    V.tensor_scalar(ohr[:, s, 0, :], iota_h[:, 0:P], e_row[d][:, bass.ds(f, 1)],
                                    e_hi[d][:, bass.ds(f, 1)], ALU.is_equal, ALU.mult)
                    last = V.tensor_scalar(ohr[:, s, 1, :], iota_h[:, 0:P], e_row[d][:, bass.ds(f, 1)],
                                           e_lo[d][:, bass.ds(f, 1)], ALU.is_equal, ALU.mult)
                last.then_inc(code_ready, 1)

            def one_hots(i, vs):
                for v in vs:
                    t = LT * i + v
                    dve.wait_ge(agg, t + 1)
                    V.tensor_scalar(oh[:, v, :], iota_h[:, 0:P], loc[:, bass.ds(t, 1)], None,
                                    ALU.is_equal).then_inc(oh_ready, 1)

            def accumulate(i, vs):
                for v in vs:
                    t = LT * i + v
                    j = dve.value_load(lbin[0:1, bass.ds(t, 1)], min_val=0, max_val=NT - 1)
                    tile = acc[:, bass.ds(j * D, D)]
                    dve.wait_ge(agg, t + 1 + LT)
                    dve.wait_ge(agg_read, t + 2)
                    V.scalar_tensor_tensor(out=tile, in0=ag[v % 3][:, :], scalar=agg_scale, in1=tile, op0=ALU.mult,
                                           op1=ALU.add).then_inc(agg_read, 1)

            def row_low(w, q, u):
                dve.wait_ge(proj_hi, NT * (w - 1) + STEPS * q + u + 1)
                V.scalar_tensor_tensor(out=trow[:, u, D:2 * D], in0=pj[u % 2][:, :], scalar=2.0 ** -14,
                                       in1=trow[:, u, 0:D], op0=ALU.mult, op1=ALU.subtract).then_inc(proj_read, 1)

            def iteration(w, par, q, d, sort, chunk):
                for u in range(STEPS):
                    codes(w, q, u, d)
                    if d == 1:
                        one_hots(ITS * (w - 1 - R) + q, PER_STEP[u])
                    if sort == "count":
                        count_bin(8 * NT + NT * par + STEPS * q + u, par, STEPS * q + u)
                    if sort == "rank":
                        rank_bin(10 * NT + 3 * (NT * par + STEPS * q + u), par, STEPS * q + u)
                    row_low(w, q, u)
                    if u == 2 and chunk:
                        w_low(par, 4 * (w + 1) + q, q)
                    if d == 1:
                        accumulate(ITS * (w - 1 - R) + q, PER_STEP[u])

            def relation(w, par, d, sort=None, chunks=True):
                with dve.Fori(0, DK) as q:
                    iteration(w, par, q, d, sort, chunks)
                iteration(w, par, DK, d, sort, False)

            def decode(d, blk):
                dve.wait_ge(perm_done, 2 * d + blk + 1)
                hi, lo = pm[0][:, 0:WIN], pm[1][:, 0:WIN]
                cols = slice(d * LTD + blk * WIN, d * LTD + (blk + 1) * WIN)
                per = float(VROWS // 2048)
                V.tensor_scalar(dec[:, 0, :], hi, -1.0, None, ALU.add)
                chain(V.tensor_scalar(dec[:, 1, :], hi, -1.0 - (per - 1) / 2, 1.0 / per, ALU.add, ALU.mult))
                chain(V.tensor_scalar(dec[:, 1, :], dec[:, 1, :], RND, None, ALU.add))
                chain(V.tensor_scalar(loc[:, cols], dec[:, 1, :], -RND, None, ALU.add))
                chain(V.scalar_tensor_tensor(out=dec[:, 1, :], in0=loc[:, cols], scalar=-per, in1=dec[:, 0, :],
                                             op0=ALU.mult, op1=ALU.add))
                V.scalar_tensor_tensor(out=gidx[:, cols], in0=dec[:, 1, :], scalar=2048.0, in1=lo, op0=ALU.mult,
                                       op1=ALU.add).then_inc(lists, 1)

            for par in range(2):
                relation(par + 1, par, 0, "count")
            dve.sem_inc(small_in, 1)
            offsets(6, lbin[:, LTD:2 * LTD])
            for par in range(2):
                relation(2 + par + 1, par, 0, "rank")
            slot_places(e_pos, e_col[1], e_row[1])
            decode(0, 0)
            with dve.Fori(2, 4) as rp:
                for par in range(2):
                    relation(2 * rp + par + 1, par, 0)
            decode(0, 1)
            dve.wait_ge(lists, 2)
            with dve.Fori(4, 6) as rp:
                for par in range(2):
                    relation(2 * rp + par + 1, par, 1)
            decode(1, 0)
            for par in range(2):
                relation(12 + par + 1, par, 1)
            relation(15, 0, 1)
            relation(16, 1, 1, chunks=False)
            decode(1, 1)
            dve.wait_ge(lists, 4)

            base = steps[0]
            with dve.Fori(0, K_BINS) as k:
                with dve.Fori(0, ITS) as q:
                    for vs in PER_STEP:
                        one_hots(LIT + ITS * k + q, vs)
                        accumulate(LIT + ITS * k + q, vs)
                dve.wait_ge(small_out, 12 + k)
                steps[0] = base
                loop_at = [0]

                def chain_k(ins):
                    loop_at[0] += 1
                    ins.then_inc(step, 1)
                    dve.wait_ge(step, base + 5 * k + loop_at[0])

                f = [exf[:, c, bass.ds(k, 1)] for c in range(12)]
                chain_k(V.tensor_scalar(f[0].bitcast(F32), pj[0][:, bass.ds(k, 1)], 1e-30, None, ALU.add))
                chain_k(V.tensor_scalar(f[1], f[0], 23, None, ALU.logical_shift_right))
                chain_k(V.tensor_scalar(f[2], f[1], 1.0, None, ALU.add))
                chain_k(V.tensor_scalar(f[4], f[2], 1, None, ALU.logical_shift_right))
                V.tensor_scalar(f[5], f[4], -1.0, 204.0, ALU.mult, ALU.add)
                chain_k(V.tensor_scalar(f[6], f[4], 41.0, None, ALU.add))
                V.tensor_scalar(f[7], f[6], 23, None, ALU.logical_shift_left)
                V.tensor_scalar(f[3], f[5], 23, None, ALU.logical_shift_left).then_inc(small_in, 1)
                dve.wait_ge(wf_hi, k + 1)
                V.scalar_tensor_tensor(out=wf[:, bass.ds(4096 * k + 2048, 2048)], in0=wfraw,
                                       scalar=f[3].bitcast(F32), in1=wf[:, bass.ds(4096 * k, 2048)],
                                       op0=ALU.mult, op1=ALU.subtract).then_inc(wf_lo, 1)
            steps[0] = base + 5 * K_BINS

            dve.wait_ge(agg_read, 2 * LTD + 2)
            with dve.Fori(0, ITS) as i:
                for u in range(STEPS):
                    j = STEPS * i + u
                    tile = acc[:, bass.ds(j * D, D)]
                    dve.wait_ge(ld_x2[u], 16 * (i + 1))
                    V.scalar_tensor_tensor(out=tile, in0=tile, scalar=0.0, in1=xin[:, u, :], op0=ALU.max,
                                           op1=ALU.add).then_inc(x1_done, 1)
                    dve.wait_ge(x1_done, j + 1)
                    last = V.bn_stats(st[:, bass.ds(j, 1), :].rearrange("p a s -> p (a s)"), tile)
            chain(V.memset(fb[:, 3, :], FAR))
            for j in range(NT):
                last = V.bn_aggr(mv[:, j, :], st[:, j, :])
            chain(last)
            norm_factors(2)

            def f_low(n, u):
                dve.wait_ge(f_hi, n + 1)
                V.tensor_tensor(trow[:, u, D:2 * D], ftmp[:, u, :], trow[:, u, 0:D], ALU.subtract).then_inc(f_lo, 1)

            normed(0, 0, ftmp, f_y)
            with dve.Fori(0, ITS - 1) as i:
                for u in range(STEPS):
                    normed(STEPS * i + u + 1, (u + 1) % 4, ftmp, f_y)
                    f_low(STEPS * i + u, u)
            for u in range(STEPS):
                if u < STEPS - 1:
                    normed(NT - STEPS + u + 1, u + 1, ftmp, f_y)
                f_low(NT - STEPS + u, u)

            xcol = acc[:, :].rearrange("p (t d) -> p t d", t=NT)[:, :, 0]
            chain(V.tensor_tensor(fb[:, 0, :], xcol, ln[:, 4, :], ALU.add))
            chain(V.tensor_tensor(fb[:, 0, :], fb[:, 0, :], ln[:, 5, :], ALU.mult))
            chain(V.tensor_copy(fb[:, 1, :], invalid[:, :]))
            for edge in BINS:
                chain(V.scalar_tensor_tensor(out=fb[:, 1, :], in0=fb[:, 0, :], scalar=edge * YS, in1=fb[:, 1, :],
                                             op0=ALU.is_gt, op1=ALU.add))
            for b in range(K_BINS):
                chain(V.tensor_scalar(fb[:, 2, :], fb[:, 1, :], float(b), None, ALU.is_equal, ALU.add,
                                      accum_out=cnt[:, b:b + 1]))
            dve.sem_inc(small_in, 1)
            offsets(19, fbin, K_BINS, 1, FT)
            for b in range(K_BINS):
                chain(V.tensor_scalar(fb[:, 2, :], fb[:, 1, :], float(b), None, ALU.is_equal))
                chain(V.tensor_tensor_scan(fb[:, 4, :], fb[:, 2, :], zeros[:, 0:NT], off[:, b:b + 1], ALU.add,
                                           ALU.add))
                chain(V.copy_predicated(fb[:, 3, :], fb[:, 2, :].bitcast(I32), fb[:, 4, :]))
            slot_places(fb[:, 3, :], fb[:, 5, :], fb[:, 6, :], fb[:, 7, :])
            for n in range(NT):
                if n >= 4:
                    dve.wait_ge(f_used, n - 3)
                V.tensor_scalar(fsc[:, n % 4, :], iota_f[:, 0:FT], fb[:, 5, n:n + 1], None, ALU.is_equal)
                V.tensor_scalar(fsa[:, n % 4, :], iota_f[:, 0:P], fb[:, 6, n:n + 1], node1f[:, n:n + 1],
                                ALU.is_equal, ALU.mult).then_inc(f_code, 1)
            dve.wait_ge(f_used, NT)
            chain(V.tensor_scalar(fd[:, 0, :], pm[0][:, 0:FT], -1.0, None, ALU.add))
            V.tensor_scalar(fgi[:, :], fd[:, 0, :], 0.0, None, ALU.max)
            chain(V.tensor_scalar(fd[:, 1, :], fd[:, 0, :], 0.0, float(2 ** 20), ALU.is_lt, ALU.mult))
            V.tensor_tensor(fsi[:, :], fd[:, 1, :], fd[:, 0, :], ALU.add).then_inc(f_idx, 1)

            def f_sum(i, u, reused):
                    t = 4 * i + u
                    kb = dve.value_load(fbin[0:1, bass.ds(t, 1)], min_val=0, max_val=K_BINS - 1)
                    dve.wait_ge(f_mm, t + 1)
                    if reused:
                        dve.wait_ge(f_out[u], 16 * i)
                    V.scalar_tensor_tensor(out=fout[:, u, :], in0=ag[u % 2][:, :],
                                           scalar=exf[:, 7, bass.ds(kb, 1)].bitcast(F32),
                                           in1=frow[:, u, 2 * D:4 * D].bitcast(F32), op0=ALU.mult,
                                           op1=ALU.add).then_inc(f_add, 1)

            for u in range(4):
                f_sum(0, u, False)
            with dve.Fori(1, FT // 4) as i:
                for u in range(4):
                    f_sum(i, u, True)


_INS = ['x', 'src', 'dst', 'edge_type_8', 'L0_gnn_W_self', 'L0_gnn_b_self', 'L0_gnn_W_rel', 'L0_gnn_b_rel', 'L0_ffn_W']


def kernel(**inputs):
    import numpy as _np
    import concourse.bacc as _bacc
    from concourse import mybir as _mybir
    from concourse.bass_utils import run_bass_kernel_spmd as _run

    nc = _bacc.Bacc("TRN2", target_bir_lowering=False, num_devices=1)
    arrays, args = {}, []
    for name in _INS:
        a = _np.ascontiguousarray(inputs[name])
        arrays[f"in_{name}"] = a
        args.append(nc.dram_tensor(f"in_{name}", a.shape, _mybir.dt.from_np(a.dtype), kind="ExternalInput").ap())
    out = nc.dram_tensor("out_0", (N, D), _mybir.dt.float32, kind="ExternalOutput").ap()
    build(nc, *args, out)
    r = _run(nc, [arrays], core_ids=[0])
    return r.results[0]["out_0"]
```

```python
import concourse.bass as bass
from concourse import mybir
from contextlib import ExitStack

F32 = mybir.dt.float32
F16 = mybir.dt.float16
I32 = mybir.dt.int32
ALU = mybir.AluOpType
ACT = mybir.ActivationFunctionType
AX_X = mybir.AxisListType.X

P = 128
N = 2500
D = 512
DK = D // P
NT = -(-N // P)
NPAD = NT * P
LAST = N - (NT - 1) * P
R = 8
NW = 2 * R + 1
SELF = NW - 1
E = 80000
EC = E // P
STEPS = 4
ITS = NT // STEPS
PERM_STEPS = [[4, 5, 4, 5], [4, 4, 4, 4]]
SLOTS = 9
ECP = 640
GT = 2
BLOCKS = [[(0, 360, 398), (360, 270, 304)], [(0, 320, 358), (320, 320, 344)]]
BC = 360
WIN = 398
LTD = 702
LT = 18
LIT = LTD // LT
VROWS = R * NPAD
K_BINS = 8
FT = 28
BINS = [-1.5, -1.0, -0.5, 0.0, 0.5, 1.0, 1.5]
RND = 12582912.0
YS = 512.0
FAR = -20000.0
assert EC * P == E and STEPS * ITS == NT and LIT * LT == LTD and LIT < R * ITS
for blocks in BLOCKS:
    assert sum(w for _, _, w in blocks) == LTD and blocks[-1][0] + blocks[-1][1] >= EC
    assert all((min(c0 + n, EC) - c0) * P + NT * (GT * P - 1) < (w + GT) * P for c0, n, w in blocks)
assert N + K_BINS * (P - 1) < (FT + 1) * P
CHUNK_A = LT // 2
PER_STEP = [range(0, 4), range(4, 8), range(8, 12), range(12, 18)]


def build(nc, x, src, dst, etype, w_self, b_self, w_rel, b_rel, w_ffn, out):
    ctx = ExitStack()
    with ctx:
        def sb(name, shape, dt):
            return ctx.enter_context(nc.sbuf_tensor(name, shape, dt))

        def sem(name):
            return ctx.enter_context(nc.semaphore(name))

        table = [nc.dram_tensor(f"table{d}", (VROWS, 2 * D), F16) for d in range(2)]
        rows = nc.dram_tensor("ffn_rows", (NPAD, 2 * D), I32)

        big = sb("big", [P, 36864], F16)
        yT = big[:, 0:2 * DK * NPAD].rearrange("p (h k n) -> p h k n", h=2, k=DK)
        wmov = big[:, 20480:28672].rearrange("p (b h k n) -> p b h k n", b=2, h=2, k=DK)
        wraw = [big[:, 20480 + 4096 * s:20480 + 4096 * (s + 1)].bitcast(F32) for s in range(4)]
        wf = big[:, 0:32768]
        wfraw = wraw[3]
        acc = sb("acc", [P, NT * D], F32)
        gath = sb("gath", [P, LT * 2 * D], F16)
        gf = gath[:, :].bitcast(F32)
        ytmp = gf[:, 0:4 * D].rearrange("p (s n) -> p s n", s=4)
        e0 = 4 * D
        ea = [gf[:, e0 + ECP * i:e0 + ECP * (i + 1)] for i in range(9)]
        e_src, e_dst, e_type = (a.bitcast(I32) for a in ea[0:3])
        e_bin, e_pos = ea[3], ea[4]
        e_tmp = [gf[:, ECP * i:ECP * (i + 1)].bitcast(I32) for i in range(2)]
        b0 = e0 + 9 * ECP
        braw = gf[0:64, b0:b0 + D]
        bh = gath[0:64, 2 * (b0 + D):2 * (b0 + D) + D]
        frow = gath[:, 0:4 * 4 * D].rearrange("p (s n) -> p s n", s=4)
        fyT = gath[:, 8192:8192 + 2 * 2 * D].rearrange("p (s n) -> p s n", s=2)
        fout = gath[:, 10240:10240 + 4096].bitcast(F32).rearrange("p (s n) -> p s n", s=4)
        xin = gath[:, 8192:12288].bitcast(F32).rearrange("p (s n) -> p s n", s=4)
        ftmp = gath[:, 12288:16384].bitcast(F32).rearrange("p (s n) -> p s n", s=4)

        trow = sb("trow", [P, 4, 2 * D], F16)
        wstage = sb("wstage", [P, DK, P], F32)
        bmov = sb("bmov", [P, D], F16)
        sel = sb("sel", [P, NW, P], F16)
        d2 = [sb(f"d2_{i}", [P, ECP], F16) for i in range(4)]
        e_row, e_col = [ea[5], d2[0][:, :]], [ea[6], d2[1][:, :]]
        e_hi, e_lo = [ea[7], d2[2][:, :]], [ea[8], d2[3][:, :]]
        work = sb("work", [P, 2, WIN], F32)
        ind, scan = work[:, 0, 0:BC], work[:, 1, 0:BC]
        zeros = sb("zeros", [P, BC], F16)
        ohc = sb("ohc", [P, SLOTS, WIN], F16)
        ohr = sb("ohr", [P, SLOTS, 2, P], F16)
        loc = sb("loc", [P, 2 * LTD + 4], F16)
        gidx = sb("gidx", [P, 2 * LTD], I32)
        gidr = sb("gidr", [P, LT], I32)
        oh = sb("oh", [P, LT, P], F16)
        lbin = sb("lbin", [1, 2 * LTD // GT], I32)
        iota_i = work[:, 0, :].bitcast(I32)
        tbc, ge = work[0:32, 0, 0:P], work[0:32, 1, :]
        iota_f = sb("iota_f", [P, WIN // GT], F32)
        iota_h = sb("iota_h", [P, WIN], F16)
        dif = sb("dif", [P, P], I32)
        difw = sb("difw", [P, NW], I32)
        selw = sb("selw", [P, 2, NW], F32)
        ident = sb("ident", [P, P], F32)
        ident_h = sb("ident_h", [P, P], F16)
        before = sb("before", [P, P], F32)
        ones = sb("ones", [P, P], F32)
        node1 = sb("node1", [P, NT], I32)
        node1f = sb("node1f", [P, NT], F32)
        invalid = sb("invalid", [P, NT], F32)
        ssq = sb("ssq", [P, NW + 1], F32)
        ssum = sb("ssum", [P, 1], F32)
        ex = sb("ex", [P, 12], I32)
        exf = sb("exf", [P, 12, K_BINS], I32)
        ssf = sb("ssf", [P, K_BINS], F32)
        st = sb("st", [P, NT, 6], F32)
        mv = sb("mv", [P, NT, 2], F32)
        ln = sb("ln", [P, 6, NT], F32)
        cnt = sb("cnt", [P, 2 * NT], F32)
        pre = sb("pre", [P, 2 * NT], F32)
        off = sb("off", [P, 2 * NT], F32)
        tcol = sb("tcol", [32, 4], F32)
        fb = sb("fb", [P, 8, NT], F32)
        fd = sb("fd", [P, 4, FT], F32)
        fgi = sb("fgi", [P, FT], I32)
        fsi = sb("fsi", [P, FT], I32)
        fbin = sb("fbin", [1, FT], I32)
        ohrf = ohr[:, :, :, :].rearrange("p s h n -> p (s h n)").bitcast(F32)
        fsa = ohrf[:, 0:4 * P].rearrange("p (s n) -> p s n", s=4)
        fsc = ohrf[:, 4 * P:4 * (P + FT)].rearrange("p (s n) -> p s n", s=4)

        bank = [ctx.enter_context(nc.psum_tensor(f"bank{i}", [P, D], F32)) for i in range(8)]
        pj = bank[0:2]
        wt = bank[2]
        pm = bank[3:5]
        ag = bank[5:8]

        ld_x = [sem(f"ld_x{i}") for i in range(ITS)]
        ld_edges = sem("ld_edges")
        ld_b = sem("ld_b")
        ld_sq = [sem(f"ld_sq{i}") for i in range(4)]
        ld_wc = sem("ld_wc")
        ld_wf = sem("ld_wf")
        ld_x2 = [sem(f"ld_x2{i}") for i in range(4)]
        consts_i = sem("consts_i")
        consts = sem("consts")
        pads = sem("pads")
        squares = sem("squares")
        step = sem("step")
        root = sem("root")
        small_in = sem("small_in")
        small_out = sem("small_out")
        y_ready = sem("y_ready")
        yt_mm = sem("yt_mm")
        yt_hi = sem("yt_hi")
        yt_lo = sem("yt_lo")
        wt_mm = sem("wt_mm")
        wt_hi = sem("wt_hi")
        wt_lo = sem("wt_lo")
        proj = sem("proj")
        proj_hi = sem("proj_hi")
        proj_read = sem("proj_read")
        row_out = [sem(f"row_out{i}") for i in range(4)]
        rank = sem("rank")
        code_ready = sem("code_ready")
        code_used = sem("code_used")
        perm_done = sem("perm_done")
        lists = sem("lists")
        oh_ready = sem("oh_ready")
        agg = sem("agg")
        agg_read = sem("agg_read")
        acc_zero = sem("acc_zero")
        got = [sem(f"got{i}") for i in range(LT)]
        idx_copied = sem("idx_copied")
        wf_sq = sem("wf_sq")
        wf_hi = sem("wf_hi")
        wf_lo = sem("wf_lo")
        x1_done = sem("x1_done")
        f_y = sem("f_y")
        f_hi = sem("f_hi")
        f_lo = sem("f_lo")
        f_rows = [sem(f"f_rows{i}") for i in range(4)]
        f_x1 = sem("f_x1")
        f_code = sem("f_code")
        f_used = sem("f_used")
        f_perm = sem("f_perm")
        f_idx = sem("f_idx")
        f_got = [sem(f"f_got{i}") for i in range(4)]
        f_tr = sem("f_tr")
        f_yT = sem("f_yT")
        f_mm = sem("f_mm")
        f_add = sem("f_add")
        f_out = [sem(f"f_out{i}") for i in range(4)]

        block = ctx.enter_context(nc.Block())
        w_order = list(range(1, NW)) + [0]

        def w_dram(w):
            return w_self if w == SELF else w_rel[w]

        @block.sync
        def _(sp):
            xg = x[0:(NT - 1) * P, :].rearrange("(t p) d -> p t d", p=P)
            accv = acc[:, :].rearrange("p (t d) -> p t d", t=NT)
            sp.wait_ge(pads, 1)
            for tile, edges in ((e_src, src), (e_dst, dst), (e_type, etype)):
                sp.dma_start(tile[:, 0:EC], edges.rearrange("(p f) -> p f", p=P)).then_inc(ld_edges, 16)
            for g in range(ITS):
                hi = min(STEPS * (g + 1), NT - 1)
                sp.dma_start(accv[:, STEPS * g:hi, :], xg[:, STEPS * g:hi, :]).then_inc(ld_x[g], 16)
            sp.wait_ge(pads, 2)
            sp.dma_start(accv[0:LAST, NT - 1, :], x[(NT - 1) * P:N, :]).then_inc(ld_x[ITS - 1], 16)
            for i, w in enumerate(w_order):
                if i >= 4:
                    sp.wait_ge(squares, i - 3)
                sp.dma_start(wraw[(i + 2) % 4].rearrange("p (c d) -> p c d", c=DK),
                             w_dram(w).rearrange("(c p) d -> p c d", p=P)).then_inc(ld_sq[(i + 2) % 4], 16)
                if i == 3:
                    sp.wait_ge(pads, 3)
                    for row in (0, 32):
                        sp.dma_start(braw[row + SELF:row + NW, :],
                                     b_self.rearrange("(a d) -> a d", a=1)).then_inc(ld_b, 16)
                        sp.dma_start(braw[row:row + SELF, :], b_rel).then_inc(ld_b, 16)

            def w_chunk(w, q, own=None):
                sp.wait_ge(wt_mm, 4 * w + q + 4)
                source = w_rel[bass.ds(w + 1, 1), :, bass.ds(q * P, P)].rearrange(
                    "a (c p) d -> p (a c) d", p=P) if own is None else \
                    own[:, bass.ds(q * P, P)].rearrange("(c p) d -> p c d", p=P)
                sp.dma_start(wstage[:, :, :], source).then_inc(ld_wc, 16)

            def store_rows(w, q, u, d, r):
                sp.wait_ge(proj_read, NT * w + STEPS * q + u + 3)
                sp.dma_start(table[d].ap()[bass.ds((r * NT + STEPS * q + u) * P, P), :],
                             trow[:, u, :]).then_inc(row_out[u], 16)

            def relation(w, d, own=None):
                with sp.Fori(0, DK) as q:
                    w_chunk(w, q, own)
                    for u in range(STEPS):
                        store_rows(w, q, u, d, w - R * d)
                for u in range(STEPS):
                    store_rows(w, DK, u, d, w - R * d)

            with sp.Fori(0, R) as w:
                relation(w, 0)
            with sp.Fori(R, 2 * R - 1) as w:
                relation(w, 1)
            relation(2 * R - 1, 1, w_self)

            for k in range(K_BINS):
                if k == 0:
                    sp.wait_ge(proj_read, NT * NW + 2)
                else:
                    sp.wait_ge(wf_lo, k)
                sp.dma_start(wfraw.rearrange("p (c o) -> p c o", c=DK),
                             w_ffn[k].rearrange("(c p) o -> p c o", p=P)).then_inc(ld_wf, 16)

            sp.wait_ge(agg, 2 * LTD + LT)

            def load_x(j, u, n=P):
                sp.dma_start(xin[0:n, u, :], x[bass.ds(j * P, n), :]).then_inc(ld_x2[u], 16)

            for u in range(STEPS):
                load_x(u, u)
            with sp.Fori(1, ITS - 1) as i:
                for u in range(STEPS):
                    sp.wait_ge(x1_done, STEPS * i + u - STEPS + 1)
                    load_x(STEPS * i + u, u)
            for u in range(STEPS):
                j = NT - STEPS + u
                sp.wait_ge(x1_done, j - STEPS + 1)
                load_x(j, u, P if j < NT - 1 else LAST)

            with sp.Fori(0, ITS) as i:
                for u in range(STEPS):
                    j = STEPS * i + u
                    sp.wait_ge(f_lo, j + 1)
                    sp.dma_start(rows.ap()[bass.ds(j * P, P), 0:D], trow[:, u, :].bitcast(I32)).then_inc(f_rows[u], 16)
                    sp.dma_start(rows.ap()[bass.ds(j * P, P), D:2 * D],
                                 acc[:, bass.ds(j * D, D)].bitcast(I32)).then_inc(f_x1, 16)

        @block.gpsimd
        def _(pool):
            nc.gpsimd.iota(iota_i[:, :], pattern=[[1, WIN]], base=0, channel_multiplier=0)
            nc.gpsimd.iota(dif[:, :], pattern=[[1, P]], base=0, channel_multiplier=-1)
            nc.gpsimd.iota(difw[:, :], pattern=[[1, NW]], base=0, channel_multiplier=-1)
            nc.gpsimd.iota(node1[:, :], pattern=[[P, NT]], base=1, channel_multiplier=1).then_inc(consts_i, 1)

            pool.wait_ge(y_ready, NT)
            nc.gpsimd.memset(acc[:, :], 0.0).then_inc(acc_zero, 1)

            def gather_set(i, d, which):
                v0, v1 = (0, CHUNK_A) if which == 0 else (CHUNK_A, LT)
                pool.wait_ge(agg, LT * i + v1)
                nc.gpsimd.tensor_copy(gidr[:, v0:v1], gidx[:, bass.ds(LT * i + v0, v1 - v0)]).then_inc(idx_copied, 1)
                pool.wait_ge(idx_copied, 2 * i + which + 1)
                pool.nop(nofuse=True)
                for v in range(v0, v1):
                    pool.indirect_dma_start(
                        out=gath[:, v * 2 * D:(v + 1) * 2 * D], out_offset=None, in_=table[d].ap(),
                        in_offset=bass.IndirectOffsetOnAxis(ap=gidr[:, v:v + 1], axis=0)).then_inc(got[v], 16)

            for d in range(2):
                pool.wait_ge(lists, 2 * d + 2)
                for u in range(4):
                    pool.wait_ge(row_out[u], 16 * (1 + R * ITS * (d + 1)))
                with pool.Fori(LIT * d, LIT * (d + 1)) as i:
                    for which in range(2):
                        gather_set(i, d, which)

            pool.wait_ge(f_idx, 1)
            for u in range(4):
                pool.wait_ge(f_rows[u], 16 * ITS)
            pool.wait_ge(f_x1, 16 * NT)

            def fetch(t):
                pool.indirect_dma_start(out=frow[:, t % 4, :].bitcast(I32), out_offset=None, in_=rows.ap(),
                                        in_offset=bass.IndirectOffsetOnAxis(ap=fgi[:, t:t + 1], axis=0)
                                        ).then_inc(f_got[t % 4], 16)

            def send(t):
                pool.wait_ge(f_add, t + 3)
                pool.indirect_dma_start(out=out, out_offset=bass.IndirectOffsetOnAxis(ap=fsi[:, t:t + 1], axis=0),
                                        in_=fout[:, t % 4, :], in_offset=None,
                                        bounds_check=N - 1, oob_is_err=False).then_inc(f_out[t % 4], 16)

            for t in range(4):
                fetch(t)
            for t in range(FT):
                send(t)
                if t + 4 < FT:
                    fetch(t + 4)
            for u in range(4):
                pool.wait_ge(f_out[u], 16 * (FT // 4))

        @block.scalar
        def _(act):
            nc.scalar.sem_inc(agg_read, 3)
            nc.scalar.sem_inc(f_yT, 2)
            for i, w in enumerate(w_order):
                act.wait_ge(ld_sq[(i + 2) % 4], 16 * (i // 4 + 1))
                if i == 0:
                    act.wait_ge(pads, 3)
                if i:
                    act.wait_ge(squares, i)
                nc.scalar.activation(trow[:, 0:2, :].rearrange("p s n -> p (s n)"), wraw[(i + 2) % 4], ACT.Square,
                                     accum_out=ssq[:, w:w + 1]).then_inc(squares, 1)
                if i == 5:
                    act.wait_ge(root, 1)
                    nc.scalar.activation(ln[:, 1, :], ln[:, 0, :], ACT.Sqrt).then_inc(root, 1)
                if i == 10:
                    with act.Fori(0, NT // 2) as j:
                        for u in range(2):
                            act.wait_ge(yt_mm, 2 * j + u + 1)
                            nc.scalar.copy(yT[:, 0, :, bass.ds((2 * j + u) * P, P)],
                                           pj[u][:, :].rearrange("p (k n) -> p k n", k=DK)).then_inc(yt_hi, 1)
            act.wait_ge(ld_b, 64)
            nc.scalar.activation(trow[0:NW, 2, 0:D], braw[0:NW, :], ACT.Square, scale=1.0 / 32,
                                 accum_out=ssq[0:NW, NW:NW + 1]).then_inc(squares, 1)

            def w_high(buf, c, q):
                act.wait_ge(wt_mm, c + 1)
                nc.scalar.activation(wmov[:, buf, 0, q, :] if isinstance(q, int) else
                                     wmov[:, buf, 0].rearrange("p k n -> p (k n)")[:, bass.ds(q * D, D)],
                                     wt[:, :], ACT.Copy, scale=ex[:, 3:4].bitcast(F32)).then_inc(wt_hi, 1)

            act.wait_ge(small_in, 7)
            for q in range(DK):
                w_high(0, q, q)
            act.wait_ge(squares, NW + 1)

            def row_high(w, q, u):
                act.wait_ge(proj, NT * w + STEPS * q + u + 1)
                act.wait_ge(row_out[u], 16 * (ITS * w + q + 1))
                nc.scalar.activation(trow[:, u, 0:D], pj[u % 2][:, :], ACT.Copy,
                                     scale=2.0 ** -14).then_inc(proj_hi, 1)

            def relation(w, nxt):
                with act.Fori(0, DK) as q:
                    for u in range(STEPS):
                        row_high(w, q, u)
                        if u == 2:
                            w_high(nxt, 4 * (w + 1) + q, q)
                for u in range(STEPS):
                    row_high(w, DK, u)

            with act.Fori(0, R) as pair:
                for par in range(2):
                    relation(2 * pair + par, 1 - par)

            for u in range(4):
                act.wait_ge(row_out[u], 16 * (1 + 2 * R * ITS))
            for k in range(K_BINS):
                act.wait_ge(ld_wf, 16 * (k + 1))
                if k:
                    act.wait_ge(wf_sq, k)
                nc.scalar.activation(trow[:, 0:2, :].rearrange("p s n -> p (s n)"), wfraw, ACT.Square,
                                     accum_out=ssf[:, k:k + 1]).then_inc(wf_sq, 1)
                act.wait_ge(small_in, 13 + k)
                nc.scalar.activation(wf[:, 4096 * k:4096 * k + 2048], wfraw, ACT.Copy,
                                     scale=exf[:, 3, k:k + 1].bitcast(F32)).then_inc(wf_hi, 1)

            act.wait_ge(wf_sq, K_BINS)
            act.wait_ge(root, 3)
            nc.scalar.activation(ln[:, 1, :], ln[:, 0, :], ACT.Sqrt).then_inc(root, 1)
            for u in range(STEPS):
                act.wait_ge(f_y, u + 1)
                nc.scalar.copy(trow[:, u, 0:D], ftmp[:, u, :]).then_inc(f_hi, 1)
            with act.Fori(1, ITS) as i:
                for u in range(STEPS):
                    act.wait_ge(f_y, STEPS * i + u + 1)
                    act.wait_ge(f_rows[u], 16 * i)
                    nc.scalar.copy(trow[:, u, 0:D], ftmp[:, u, :]).then_inc(f_hi, 1)

            with act.Fori(0, FT // 4) as i:
                for u in range(4):
                    act.wait_ge(f_tr, 4 * i + u + 1)
                    nc.scalar.copy(fyT[:, u % 2, :], pj[u % 2][:, :].bitcast(F16)).then_inc(f_yT, 1)

        @block.tensor
        def _(pe):
            nc.tensor.sem_inc(code_used, 2)
            nc.tensor.sem_inc(agg, LT)

            pe.wait_ge(consts, 1)

            def small(outp, lhsT, rhs):
                return nc.tensor.matmul(outp, lhsT, rhs, start=True, stop=True)


            def offsets(base, n_bins=NT, wins=None, d=0):
                wins = wins or [w // GT for _, _, w in BLOCKS[d]]
                blocks = len(wins)
                pe.wait_ge(small_in, base)
                small(ag[0][:, 0:blocks * n_bins], before[:, :], cnt[:, 0:blocks * n_bins])
                for b in range(blocks):
                    mm = small(ag[1][0:n_bins, b:b + 1], cnt[:, b * n_bins:(b + 1) * n_bins], ones[:, 0:1])
                mm.then_inc(small_out, 1)
                for b in range(blocks):
                    pe.wait_ge(small_in, base + 1 + 2 * b)
                    small(ag[0][:, 0:n_bins], tbc[0:n_bins, :], before[0:n_bins, 0:n_bins])
                    small(ag[1][0:n_bins, 0:1], before[0:n_bins, 0:n_bins], tcol[0:n_bins, b:b + 1]
                          ).then_inc(small_out, 1)
                    pe.wait_ge(small_in, base + 2 + 2 * b)
                    small(ag[2][0:1, 0:wins[b]], ones[0:n_bins, 0:1], ge[0:n_bins, 0:wins[b]]).then_inc(small_out, 1)

            offsets(1)

            with pe.Fori(0, NT // 4) as i:
                for u in range(4):
                    pe.wait_ge(y_ready, 4 * i + u + 1)
                    pe.wait_ge(yt_lo, 4 * i + u + 1)
                    for k in range(DK):
                        mm = nc.tensor.transpose(pj[u % 2][:, k * P:(k + 1) * P], ytmp[:, u, k * P:(k + 1) * P],
                                                 ident[:, :])
                    mm.then_inc(yt_mm, 1)

            pe.wait_ge(small_in, 6)
            small(ag[0][:, 0:1], ones[:, :], ssum[:, :]).then_inc(small_out, 1)

            def w_transpose(c, raw):
                pe.wait_ge(wt_lo, c + 1)
                for oc in range(DK):
                    mm = nc.tensor.transpose(wt[:, oc * P:(oc + 1) * P], raw[oc], ident[:, :])
                mm.then_inc(wt_mm, 1)

            pe.wait_ge(ld_sq[(NW - 1 + 2) % 4], 16 * ((NW - 1) // 4 + 1))
            raw0 = wraw[(NW - 1 + 2) % 4]
            for q in range(DK):
                w_transpose(q, [raw0[:, oc * D + q * P:oc * D + (q + 1) * P] for oc in range(DK)])
            stage = [wstage[:, oc, :] for oc in range(DK)]

            def project(w, buf, q, u):
                j = STEPS * q + u
                pe.wait_ge(proj_read, NT * w + j + 1)
                pe.nop(nofuse=True)
                ps = pj[u % 2][:, :]
                nc.tensor.matmul(ps, sel[:, :, :].rearrange("p w n -> p (w n)")[:, bass.ds(w * P, P)], bmov[:, :],
                                 start=True, stop=False)
                for k in range(DK):
                    yh = big[:, bass.ds(k * NPAD + j * P, P)]
                    yl = big[:, bass.ds((DK + k) * NPAD + j * P, P)]
                    nc.tensor.matmul(ps, yh, wmov[:, buf, 0, k, :], start=False, stop=False)
                    nc.tensor.matmul(ps, yh, wmov[:, buf, 1, k, :], start=False, stop=False)
                    mm = nc.tensor.matmul(ps, yl, wmov[:, buf, 0, k, :], start=False, stop=(k == DK - 1))
                mm.then_inc(proj, 1)

            def permute(w, q, u, d, win):
                pe.wait_ge(code_ready, NT * (w - 1) + STEPS * q + u + 1)
                for v in range(PERM_STEPS[d][u]):
                    s = (u % 2) * 4 + v
                    for h in range(2):
                        mm = nc.tensor.matmul(pm[h][:, 0:win], ohr[:, s, h, :], ohc[:, s, 0:win], start=False,
                                              stop=False, skip_group_check=True)
                mm.then_inc(code_used, 1)

            def open_block(n, win):
                if n:
                    pe.wait_ge(lists, n)
                for h in range(2):
                    nc.tensor.matmul(pm[h][:, 0:win], zeros[:, 0:P], iota_h[:, 0:win], start=True,
                                     stop=False, skip_group_check=True)

            def close_block(win):
                for h in range(2):
                    mm = nc.tensor.matmul(pm[h][:, 0:win], zeros[:, 0:P], iota_h[:, 0:win], start=False,
                                          stop=True, skip_group_check=True)
                mm.then_inc(perm_done, 1)

            def sum_tiles(i, vs):
                for v in vs:
                    t = LT * i + v
                    ps = ag[v // GT % 3][:, :]
                    if v % GT == 0:
                        pe.wait_ge(oh_ready, t + GT)
                        pe.wait_ge(agg_read, LT // GT * i + v // GT + 1)
                    pe.wait_ge(got[v], 16 * (i + 1))
                    nc.tensor.matmul(ps, oh[:, v, :], gath[:, v * 2 * D:v * 2 * D + D], start=(v % GT == 0),
                                     stop=False)
                    nc.tensor.matmul(ps, oh[:, v, :], gath[:, v * 2 * D + D:(v + 1) * 2 * D], start=False,
                                     stop=(v % GT == GT - 1)).then_inc(agg, 1)

            def iteration(w, buf, q, chunk=True, perm=None, summing=None):
                for u in range(STEPS):
                    project(w, buf, q, u)
                    if u == 2 and chunk:
                        pe.wait_ge(ld_wc, 16 * (4 * w + q + 1))
                        w_transpose(4 * (w + 1) + q, stage)
                    if summing is not None:
                        sum_tiles(summing, PER_STEP[u])
                    if perm:
                        permute(w, q, u, *perm)

            def relation(w, par, perm=None, summing=False, last=False):
                pe.wait_ge(wt_lo, 4 * (w + 1) + 1)
                pe.nop(nofuse=True)
                with pe.Fori(0, DK) as q:
                    iteration(w, par, q, True, perm, ITS * (w - R) + q if summing else None)
                iteration(w, par, DK, False, perm, ITS * (w - R) + DK if summing and not last else None)

            pe.wait_ge(yt_lo, NT + 2)
            relation(0, 0)
            (_, _, win0), (_, _, win1) = BLOCKS[0]
            open_block(0, win0)
            relation(1, 1, (0, win0))
            relation(2, 0, (0, win0))
            relation(3, 1, (0, win0))
            relation(4, 0, (0, win0))
            close_block(win0)
            open_block(1, win1)
            for w in range(5, R):
                relation(w, w % 2, (0, win1))
                if w == 5:
                    offsets(8, d=1)
            close_block(win1)
            (_, _, win0), (_, _, win1) = BLOCKS[1]
            open_block(2, win0)
            with pe.Fori(R // 2, R // 2 + 2) as rp:
                for par in range(2):
                    relation(2 * rp + par, par, (1, win0), True)
            close_block(win0)
            open_block(3, win1)
            for w in range(12, 2 * R):
                relation(w, w % 2, (1, win1), True, w == 2 * R - 1)
            close_block(win1)

            pe.wait_ge(wt_lo, 4 * NW + 1)
            with pe.Fori(0, ITS) as q:
                iteration(SELF, 0, q, False, None, LIT + q)
            with pe.Fori(0, K_BINS) as k:
                with pe.Fori(0, 4) as q:
                    for vs in PER_STEP:
                        sum_tiles(LIT + ITS + 4 * k + q, vs)
                pe.wait_ge(wf_sq, k + 1)
                pe.wait_ge(small_in, 12 + k)
                small(pj[0][:, 0:K_BINS], ones[:, :], ssf[:, :]).then_inc(small_out, 1)
            with pe.Fori(LIT + ITS + 4 * K_BINS, 2 * LIT) as i:
                for vs in PER_STEP:
                    sum_tiles(i, vs)

            offsets(21, K_BINS, [FT])
            for n in range(NT):
                pe.wait_ge(f_code, n + 1)
                nc.tensor.matmul(pm[0][:, 0:FT], fsa[:, n % 4, :], fsc[:, n % 4, :], start=(n == 0),
                                 stop=(n == NT - 1)).then_inc(f_used, 1)

            def f_transpose(m, slot, uses):
                pe.wait_ge(f_got[slot], 16 * uses)
                pe.wait_ge(f_yT, m + 1)
                for c in range(2 * DK):
                    mm = nc.tensor.transpose(pj[slot % 2][:, :].bitcast(F16)[:, c * P:(c + 1) * P],
                                             frow[:, slot, c * P:(c + 1) * P], ident_h[:, :])
                mm.then_inc(f_tr, 1)

            def f_product(t, slot):
                pe.wait_ge(f_yT, t + 3)
                pe.wait_ge(f_add, t + 1)
                pe.nop(nofuse=True)
                kb = pe.value_load(fbin[0:1, bass.ds(t, 1)], min_val=0, max_val=K_BINS - 1)
                ps = ag[slot % 2][:, :]
                for k in range(DK):
                    wh = wf[:, bass.ds(kb * 4096 + k * D, D)]
                    wl = wf[:, bass.ds(kb * 4096 + 2048 + k * D, D)]
                    yh = fyT[:, slot % 2, k * P:(k + 1) * P]
                    yl = fyT[:, slot % 2, (DK + k) * P:(DK + k + 1) * P]
                    nc.tensor.matmul(ps, yh, wh, start=(k == 0), stop=False)
                    nc.tensor.matmul(ps, yh, wl, start=False, stop=False)
                    mm = nc.tensor.matmul(ps, yl, wh, start=False, stop=(k == DK - 1))
                mm.then_inc(f_mm, 1)

            pe.wait_ge(wf_lo, K_BINS)
            pe.wait_ge(f_idx, 1)
            f_transpose(0, 0, 1)
            with pe.Fori(0, FT // 4 - 1) as i:
                for u in range(4):
                    f_transpose(4 * i + u + 1, (u + 1) % 4, i + 1 + (u == 3))
                    f_product(4 * i + u, u)
            for u in range(4):
                t = FT - 4 + u
                if u < 3:
                    f_transpose(t + 1, u + 1, FT // 4)
                f_product(t, u)

        @block.vector
        def _(dve):
            V = nc.vector
            V.sem_inc(yt_lo, 2)
            V.sem_inc(wt_lo, 1)
            V.sem_inc(proj_read, 2)
            V.sem_inc(f_add, 2)
            for u in range(4):
                V.sem_inc(row_out[u], 16)
            steps = [0]

            def chain(ins):
                steps[0] += 1
                ins.then_inc(step, 1)
                dve.wait_ge(step, steps[0])

            V.memset(e_src[:, EC:ECP], NPAD)
            V.memset(e_dst[:, EC:ECP], NPAD)
            V.memset(e_type[:, EC:ECP], 0).then_inc(pads, 1)
            V.memset(acc[:, (NT - 1) * D:NT * D], 0.0).then_inc(pads, 1)
            V.memset(ssq[:, :], 0.0)
            V.memset(braw, 0.0).then_inc(pads, 1)

            V.memset(ones[:, :], 1.0)
            V.memset(zeros[:, :], 0.0)
            V.memset(bmov[:, :], 0.0)
            chain(V.memset(ssf[:, :], 0.0))
            dve.wait_ge(consts_i, 1)
            V.tensor_copy(iota_f[:, :], iota_i[:, 0:WIN // GT])
            V.tensor_copy(iota_h[:, :], iota_i[:, :])
            V.tensor_scalar(ident_h[:, :], dif[:, :], 0.0, None, ALU.is_equal)
            V.tensor_scalar(before[:, :], dif[:, :], 0.0, None, ALU.is_gt)
            V.tensor_copy(node1f[:, :], node1[:, :])
            V.tensor_scalar(invalid[:, :], node1[:, :], float(N), -100.0, ALU.is_gt, ALU.mult)
            V.tensor_scalar(selw[:, 0, :], difw[:, :], 0.0, 2.0 ** 13, ALU.is_equal, ALU.mult)
            V.tensor_scalar(selw[:, 1, :], difw[:, :], -32.0, 2.0 ** 13, ALU.is_equal, ALU.mult)
            V.tensor_scalar(ident[:, :], dif[:, :], 0.0, None, ALU.is_equal).then_inc(consts, 1)
            dve.wait_ge(consts, 1)
            chain(V.tensor_tensor(selw[:, 0, :], selw[:, 0, :], selw[:, 1, :], ALU.add))
            for w in range(NW):
                last = V.tensor_scalar(sel[:, w, :], ones[:, :], selw[:, 0, w:w + 1], None, ALU.mult)
            chain(last)

            dve.wait_ge(ld_edges, 48)

            def prepare(d):
                node, other = (e_src, e_dst) if d == 0 else (e_dst, e_src)
                a, b = e_tmp
                chain(V.tensor_scalar(a, node, 7, None, ALU.logical_shift_right))
                chain(V.tensor_copy(e_bin, a))
                chain(V.scalar_tensor_tensor(out=a, in0=e_type, scalar=float(NPAD), in1=other, op0=ALU.mult,
                                             op1=ALU.add))
                chain(V.tensor_scalar(b, a, 11, None, ALU.logical_shift_right))
                chain(V.tensor_scalar(e_pos.bitcast(I32), a, 2047, None, ALU.bitwise_and))
                chain(V.tensor_copy(e_lo[d][:, :], e_pos.bitcast(I32)))
                chain(V.tensor_scalar(a, node, P - 1, None, ALU.bitwise_and))
                chain(V.scalar_tensor_tensor(out=e_hi[d][:, :], in0=a, scalar=float(VROWS // 2048), in1=b, op0=ALU.mult,
                                             op1=ALU.add))
                chain(V.tensor_scalar(e_hi[d][:, :], e_hi[d][:, :], 1.0, None, ALU.add))
                chain(V.memset(e_pos, FAR))

            def edge_cols(d, blk):
                return slice(BLOCKS[d][blk][0], BLOCKS[d][blk][0] + BLOCKS[d][blk][1])

            def count_bin(m, d, blk, b):
                cols = edge_cols(d, blk)
                V.tensor_scalar((ind, scan)[blk][:, 0:BLOCKS[d][blk][1]], e_bin[:, cols], iota_f[:, bass.ds(b, 1)],
                                None, ALU.is_equal, ALU.add,
                                accum_out=cnt[:, bass.ds(blk * NT + b, 1)]).then_inc(rank, 1)
                dve.wait_ge(rank, m + 1)

            def rank_bin(m, d, blk, b):
                cols, n = edge_cols(d, blk), BLOCKS[d][blk][1]
                V.tensor_scalar(ind[:, 0:n], e_bin[:, cols], iota_f[:, bass.ds(b, 1)], None,
                                ALU.is_equal).then_inc(rank, 1)
                dve.wait_ge(rank, m + 1)
                V.tensor_tensor_scan(scan[:, 0:n], ind[:, 0:n], zeros[:, 0:n], off[:, bass.ds(blk * NT + b, 1)],
                                     ALU.add, ALU.add).then_inc(rank, 1)
                dve.wait_ge(rank, m + 2)
                dve.nop(nofuse=True)
                V.copy_predicated(e_pos[:, cols], ind[:, 0:n].bitcast(I32), scan[:, 0:n]).then_inc(rank, 1)
                dve.wait_ge(rank, m + 3)

            def offsets(out0, bins_out, n_bins, wins, tiles):
                blocks, group = len(wins), float(tiles * P)
                dve.wait_ge(small_out, out0 + 1)
                chain(V.tensor_scalar(pre[:, 0:blocks * n_bins], ag[0][:, 0:blocks * n_bins], -1.0, None, ALU.add))
                t = tcol[0:n_bins, 0:blocks]
                chain(V.tensor_scalar(t, ag[1][0:n_bins, 0:blocks], (group - 1) / 2, 1.0 / group, ALU.add, ALU.mult))
                chain(V.tensor_scalar(t, t, RND, None, ALU.add))
                chain(V.tensor_scalar(t, t, -RND, None, ALU.add))
                for b in range(blocks):
                    cols = slice(b * n_bins, (b + 1) * n_bins)
                    V.tensor_scalar(tbc[0:n_bins, :], ones[0:n_bins, :], tcol[0:n_bins, b:b + 1], None,
                                    ALU.mult).then_inc(small_in, 1)
                    dve.wait_ge(small_out, out0 + 2 + 2 * b)
                    chain(V.scalar_tensor_tensor(out=off[:, cols], in0=ag[0][:, 0:n_bins], scalar=group,
                                                 in1=pre[:, cols], op0=ALU.mult, op1=ALU.add))
                    V.tensor_scalar(ge[0:n_bins, 0:wins[b]], iota_f[0:n_bins, 0:wins[b]], ag[1][0:n_bins, 0:1], None,
                                    ALU.is_ge).then_inc(small_in, 1)
                    dve.wait_ge(small_out, out0 + 3 + 2 * b)
                    chain(V.tensor_scalar(bins_out[:, sum(wins[:b]):sum(wins[:b + 1])], ag[2][0:1, 0:wins[b]], -1.0,
                                          None, ALU.add))

            def slot_places(pos, col, row, tmp=None):
                tmp = e_tmp[0].bitcast(F32)[:, 0:pos.shape[1]] if tmp is None else tmp
                chain(V.tensor_scalar(tmp, pos, -63.5, 1.0 / P, ALU.add, ALU.mult))
                chain(V.tensor_scalar(tmp, tmp, RND, None, ALU.add))
                chain(V.tensor_scalar(col, tmp, -RND, None, ALU.add))
                chain(V.scalar_tensor_tensor(out=row, in0=col, scalar=-float(P), in1=pos, op0=ALU.mult, op1=ALU.add))

            prepare(0)
            with dve.Fori(0, NT) as b:
                for blk in range(2):
                    count_bin(2 * b + blk, 0, blk, b)
            dve.sem_inc(small_in, 1)
            offsets(0, lbin[:, 0:LTD // GT], NT, [w // GT for _, _, w in BLOCKS[0]], GT)

            def norm_factors(at):
                V.tensor_scalar(ln[:, 0, :], mv[:, :, 1], 1e-5, None, ALU.add).then_inc(root, 1)
                dve.wait_ge(root, at + 2)
                chain(V.reciprocal(ln[:, 2, :], ln[:, 1, :]))
                chain(V.tensor_tensor(ln[:, 3, :], ln[:, 0, :], ln[:, 2, :], ALU.mult))
                chain(V.tensor_tensor(ln[:, 2, :], ln[:, 1, :], ln[:, 3, :], ALU.add))
                chain(V.tensor_scalar(ln[:, 3, :], ln[:, 2, :], 0.5, None, ALU.mult))
                chain(V.reciprocal(ln[:, 2, :], ln[:, 3, :]))
                V.tensor_scalar(ln[:, 5, :], ln[:, 2, :], YS, None, ALU.mult)
                chain(V.tensor_scalar(ln[:, 4, :], mv[:, :, 0], -1.0, None, ALU.mult))

            for g in range(ITS):
                dve.wait_ge(ld_x[g], 32 if g == ITS - 1 else 16)
                for j in range(STEPS * g, STEPS * (g + 1)):
                    last = V.bn_stats(st[:, j, :], acc[:, j * D:(j + 1) * D])
            chain(last)
            for j in range(NT):
                last = V.bn_aggr(mv[:, j, :], st[:, j, :])
            chain(last)
            norm_factors(0)

            def normed(n, u, tile, done):
                V.tensor_scalar(tile[:, u, :], acc[:, bass.ds(n * D, D)], ln[:, 4, bass.ds(n, 1)],
                                ln[:, 5, bass.ds(n, 1)], ALU.add, ALU.mult).then_inc(done, 1)

            def y_low(n, u):
                dve.wait_ge(yt_hi, n + 1)
                V.tensor_tensor(yT[:, 1, :, bass.ds(n * P, P)], pj[u % 2][:, :].rearrange("p (k n) -> p k n", k=DK),
                                yT[:, 0, :, bass.ds(n * P, P)], ALU.subtract).then_inc(yt_lo, 1)

            for n in range(2):
                normed(n, n, ytmp, y_ready)
            with dve.Fori(0, ITS - 1) as i:
                for u in range(STEPS):
                    normed(STEPS * i + u + 2, (u + 2) % 4, ytmp, y_ready)
                    y_low(STEPS * i + u, u)
            for u in range(STEPS):
                if u < 2:
                    normed(NT - STEPS + u + 2, u + 2, ytmp, y_ready)
                y_low(NT - STEPS + u, u)

            def scales(total, e, extra=False):
                f = [e(c) for c in range(12)]
                chain(V.tensor_scalar(f[0].bitcast(F32), total, 1e-30, None, ALU.add))
                chain(V.tensor_scalar(f[1], f[0], 23, None, ALU.logical_shift_right))
                chain(V.tensor_scalar(f[2], f[1], 1.0, None, ALU.add))
                chain(V.tensor_scalar(f[4], f[2], 1, None, ALU.logical_shift_right))
                V.tensor_scalar(f[5], f[4], -1.0, 204.0, ALU.mult, ALU.add)
                V.tensor_scalar(f[8], f[4], 55.0, None, ALU.add)
                V.tensor_scalar(f[10], f[4], -1.0, 200.0, ALU.mult, ALU.add)
                chain(V.tensor_scalar(f[6], f[4], 41.0, None, ALU.add))
                V.tensor_scalar(f[3], f[5], 23, None, ALU.logical_shift_left)
                V.tensor_scalar(f[9], f[8], 23, None, ALU.logical_shift_left)
                V.tensor_scalar(f[11], f[10], 23, None, ALU.logical_shift_left)
                return V.tensor_scalar(f[7], f[6], 23, None, ALU.logical_shift_left)

            dve.wait_ge(squares, NW + 1)
            V.tensor_reduce(ssum[:, :], ssq[:, :], AX_X, ALU.add).then_inc(small_in, 1)
            dve.wait_ge(small_out, 6)
            chain(scales(ag[0][:, 0:1], lambda c: ex[:, c:c + 1]))
            w_scale = ex[:, 3:4].bitcast(F32)
            self_scale = ex[:, 7:8].bitcast(F32)
            agg_scale = ex[:, 9:10].bitcast(F32)
            dve.wait_ge(ld_b, 64)
            chain(V.tensor_scalar(braw, braw, ex[0:64, 11:12].bitcast(F32), None, ALU.mult))
            chain(V.tensor_copy(bh, braw))
            V.tensor_copy(bmov[0:32, :], bh[0:32, :])
            V.tensor_tensor(bmov[32:64, :], braw[32:64, :], bh[32:64, :], ALU.subtract).then_inc(small_in, 1)

            def w_low(buf, c, q):
                dve.wait_ge(wt_hi, c + 1)
                V.scalar_tensor_tensor(
                    out=wmov[:, buf, 1].rearrange("p k n -> p (k n)")[:, bass.ds(q * D, D)], in0=wt[:, :],
                    scalar=w_scale, in1=wmov[:, buf, 0].rearrange("p k n -> p (k n)")[:, bass.ds(q * D, D)],
                    op0=ALU.mult, op1=ALU.subtract).then_inc(wt_lo, 1)

            for q in range(DK):
                w_low(0, q, q)

            def codes(w, q, u, d, win):
                ps = NT * (w - 1) + STEPS * q + u
                first = (ITS * (w - (1, R)[d]) + q) * sum(PERM_STEPS[d]) + sum(PERM_STEPS[d][:u])
                dve.wait_ge(code_used, ps + 1)
                for v in range(PERM_STEPS[d][u]):
                    s = (u % 2) * 4 + v
                    f = first + v
                    V.tensor_scalar(ohc[:, s, 0:win], iota_h[:, 0:win], e_col[d][:, bass.ds(f, 1)], None, ALU.is_equal)
                    V.tensor_scalar(ohr[:, s, 0, :], iota_h[:, 0:P], e_row[d][:, bass.ds(f, 1)],
                                    e_hi[d][:, bass.ds(f, 1)], ALU.is_equal, ALU.mult)
                    last = V.tensor_scalar(ohr[:, s, 1, :], iota_h[:, 0:P], e_row[d][:, bass.ds(f, 1)],
                                           e_lo[d][:, bass.ds(f, 1)], ALU.is_equal, ALU.mult)
                last.then_inc(code_ready, 1)

            def one_hots(i, vs):
                for v in vs:
                    t = LT * i + v
                    dve.wait_ge(agg, t + 1)
                    V.tensor_scalar(oh[:, v, :], iota_h[:, 0:P], loc[:, bass.ds(t, 1)], None,
                                    ALU.is_equal).then_inc(oh_ready, 1)

            def accumulate(i, vs):
                for v in vs[::GT]:
                    g = LT // GT * i + v // GT
                    j = dve.value_load(lbin[0:1, bass.ds(g, 1)], min_val=0, max_val=NT - 1)
                    tile = acc[:, bass.ds(j * D, D)]
                    dve.wait_ge(agg, LT * i + v + GT + LT)
                    dve.wait_ge(agg_read, g + 3)
                    V.scalar_tensor_tensor(out=tile, in0=ag[v // GT % 3][:, :], scalar=agg_scale, in1=tile,
                                           op0=ALU.mult, op1=ALU.add).then_inc(agg_read, 1)

            def row_low(w, q, u):
                dve.wait_ge(proj_hi, NT * w + STEPS * q + u + 1)
                V.scalar_tensor_tensor(out=trow[:, u, D:2 * D], in0=pj[u % 2][:, :], scalar=2.0 ** -14,
                                       in1=trow[:, u, 0:D], op0=ALU.mult, op1=ALU.subtract).then_inc(proj_read, 1)

            def iteration(w, par, q, perm, sort, chunk, summing):
                for u in range(STEPS):
                    b = STEPS * q + u
                    if perm is not None:
                        codes(w, q, u, *perm)
                    if summing:
                        one_hots(ITS * (w - R) + q, PER_STEP[u])
                    if sort == "rank 0":
                        for blk in range(2):
                            rank_bin(2 * NT + 6 * b + 3 * blk, 0, blk, b)
                    if sort == "count 1":
                        for blk in range(2):
                            count_bin(8 * NT + 2 * b + blk, 1, blk, b)
                    if sort in ("rank 1, block 0", "rank 1, block 1"):
                        blk = int(sort == "rank 1, block 1")
                        rank_bin(10 * NT + 3 * (NT * blk + b), 1, blk, b)
                    row_low(w, q, u)
                    if u == 2 and chunk:
                        w_low(1 - par, 4 * (w + 1) + q, q)
                    if summing:
                        accumulate(ITS * (w - R) + q, PER_STEP[u])

            def relation(w, par, perm=None, sort=None, summing=False, last=False):
                with dve.Fori(0, DK) as q:
                    iteration(w, par, q, perm, sort, True, summing)
                iteration(w, par, DK, perm, sort, False, summing and not last)

            def decode(d, blk):
                dve.wait_ge(perm_done, 2 * d + blk + 1)
                win = BLOCKS[d][blk][2]
                start = d * LTD + blk * BLOCKS[d][0][2]
                hi, lo = pm[0][:, 0:win], pm[1][:, 0:win]
                whole, part = work[:, 0, 0:win], work[:, 1, 0:win]
                cols = slice(start, start + win)
                per = float(VROWS // 2048)
                V.tensor_scalar(whole, hi, -1.0, None, ALU.add)
                chain(V.tensor_scalar(part, hi, -1.0 - (per - 1) / 2, 1.0 / per, ALU.add, ALU.mult))
                chain(V.tensor_scalar(part, part, RND, None, ALU.add))
                chain(V.tensor_scalar(loc[:, cols], part, -RND, None, ALU.add))
                chain(V.scalar_tensor_tensor(out=part, in0=loc[:, cols], scalar=-per, in1=whole, op0=ALU.mult,
                                             op1=ALU.add))
                V.scalar_tensor_tensor(out=gidx[:, cols], in0=part, scalar=2048.0, in1=lo, op0=ALU.mult,
                                       op1=ALU.add).then_inc(lists, 1)

            relation(0, 0, sort="rank 0")
            slot_places(e_pos, e_col[0], e_row[0])
            for w in range(1, 5):
                relation(w, w % 2, (0, BLOCKS[0][0][2]))
            decode(0, 0)
            prepare(1)
            relation(5, 1, (0, BLOCKS[0][1][2]), "count 1")
            dve.sem_inc(small_in, 1)
            offsets(6, lbin[:, LTD // GT:2 * LTD // GT], NT, [w // GT for _, _, w in BLOCKS[1]], GT)
            relation(6, 0, (0, BLOCKS[0][1][2]), "rank 1, block 0")
            relation(7, 1, (0, BLOCKS[0][1][2]), "rank 1, block 1")
            slot_places(e_pos, e_col[1], e_row[1])
            decode(0, 1)
            dve.wait_ge(lists, 2)
            dve.wait_ge(acc_zero, 1)

            with dve.Fori(R // 2, R // 2 + 2) as rp:
                for par in range(2):
                    relation(2 * rp + par, par, (1, BLOCKS[1][0][2]), summing=True)
            decode(1, 0)
            for w in range(12, 2 * R):
                relation(w, w % 2, (1, BLOCKS[1][1][2]), summing=True, last=(w == 2 * R - 1))
            decode(1, 1)
            dve.wait_ge(lists, 4)

            with dve.Fori(0, ITS) as q:
                for u in range(STEPS):
                    b, groups = STEPS * q + u, LT // GT * (LIT + q) + PER_STEP[u][0] // GT
                    tile = acc[:, bass.ds(b * D, D)]
                    one_hots(LIT + q, PER_STEP[u])
                    dve.wait_ge(proj, NT * SELF + b + 1)
                    dve.wait_ge(agg_read, groups + 3)
                    V.scalar_tensor_tensor(out=tile, in0=pj[u % 2][:, :], scalar=self_scale, in1=tile, op0=ALU.mult,
                                           op1=ALU.add).then_inc(proj_read, 1)
                    dve.wait_ge(proj_read, NT * SELF + b + 3)
                    accumulate(LIT + q, PER_STEP[u])

            base = steps[0]
            with dve.Fori(0, K_BINS) as k:
                with dve.Fori(0, 4) as q:
                    for vs in PER_STEP:
                        one_hots(LIT + ITS + 4 * k + q, vs)
                        accumulate(LIT + ITS + 4 * k + q, vs)
                dve.wait_ge(small_out, 12 + k)
                steps[0] = base
                loop_at = [0]

                def chain_k(ins):
                    loop_at[0] += 1
                    ins.then_inc(step, 1)
                    dve.wait_ge(step, base + 5 * k + loop_at[0])

                f = [exf[:, c, bass.ds(k, 1)] for c in range(12)]
                chain_k(V.tensor_scalar(f[0].bitcast(F32), pj[0][:, bass.ds(k, 1)], 1e-30, None, ALU.add))
                chain_k(V.tensor_scalar(f[1], f[0], 23, None, ALU.logical_shift_right))
                chain_k(V.tensor_scalar(f[2], f[1], 1.0, None, ALU.add))
                chain_k(V.tensor_scalar(f[4], f[2], 1, None, ALU.logical_shift_right))
                V.tensor_scalar(f[5], f[4], -1.0, 204.0, ALU.mult, ALU.add)
                chain_k(V.tensor_scalar(f[6], f[4], 41.0, None, ALU.add))
                V.tensor_scalar(f[7], f[6], 23, None, ALU.logical_shift_left)
                V.tensor_scalar(f[3], f[5], 23, None, ALU.logical_shift_left).then_inc(small_in, 1)
                dve.wait_ge(wf_hi, k + 1)
                V.scalar_tensor_tensor(out=wf[:, bass.ds(4096 * k + 2048, 2048)], in0=wfraw,
                                       scalar=f[3].bitcast(F32), in1=wf[:, bass.ds(4096 * k, 2048)],
                                       op0=ALU.mult, op1=ALU.subtract).then_inc(wf_lo, 1)
            steps[0] = base + 5 * K_BINS
            with dve.Fori(LIT + ITS + 4 * K_BINS, 2 * LIT) as i:
                for vs in PER_STEP:
                    one_hots(i, vs)
                    accumulate(i, vs)

            dve.wait_ge(agg_read, 2 * LTD // GT + 3)
            with dve.Fori(0, ITS) as i:
                for u in range(STEPS):
                    j = STEPS * i + u
                    tile = acc[:, bass.ds(j * D, D)]
                    dve.wait_ge(ld_x2[u], 16 * (i + 1))
                    V.scalar_tensor_tensor(out=tile, in0=tile, scalar=0.0, in1=xin[:, u, :], op0=ALU.max,
                                           op1=ALU.add).then_inc(x1_done, 1)
                    dve.wait_ge(x1_done, j + 1)
                    last = V.bn_stats(st[:, bass.ds(j, 1), :].rearrange("p a s -> p (a s)"), tile)
            chain(V.memset(fb[:, 3, :], FAR))
            for j in range(NT):
                last = V.bn_aggr(mv[:, j, :], st[:, j, :])
            chain(last)
            norm_factors(2)

            def f_low(n, u):
                dve.wait_ge(f_hi, n + 1)
                V.tensor_tensor(trow[:, u, D:2 * D], ftmp[:, u, :], trow[:, u, 0:D], ALU.subtract).then_inc(f_lo, 1)

            normed(0, 0, ftmp, f_y)
            with dve.Fori(0, ITS - 1) as i:
                for u in range(STEPS):
                    normed(STEPS * i + u + 1, (u + 1) % 4, ftmp, f_y)
                    f_low(STEPS * i + u, u)
            for u in range(STEPS):
                if u < STEPS - 1:
                    normed(NT - STEPS + u + 1, u + 1, ftmp, f_y)
                f_low(NT - STEPS + u, u)

            xcol = acc[:, :].rearrange("p (t d) -> p t d", t=NT)[:, :, 0]
            chain(V.tensor_tensor(fb[:, 0, :], xcol, ln[:, 4, :], ALU.add))
            chain(V.tensor_tensor(fb[:, 0, :], fb[:, 0, :], ln[:, 5, :], ALU.mult))
            chain(V.tensor_copy(fb[:, 1, :], invalid[:, :]))
            for edge in BINS:
                chain(V.scalar_tensor_tensor(out=fb[:, 1, :], in0=fb[:, 0, :], scalar=edge * YS, in1=fb[:, 1, :],
                                             op0=ALU.is_gt, op1=ALU.add))
            for b in range(K_BINS):
                chain(V.tensor_scalar(fb[:, 2, :], fb[:, 1, :], float(b), None, ALU.is_equal, ALU.add,
                                      accum_out=cnt[:, b:b + 1]))
            dve.sem_inc(small_in, 1)
            offsets(19, fbin, K_BINS, [FT], 1)
            for b in range(K_BINS):
                chain(V.tensor_scalar(fb[:, 2, :], fb[:, 1, :], float(b), None, ALU.is_equal))
                chain(V.tensor_tensor_scan(fb[:, 4, :], fb[:, 2, :], zeros[:, 0:NT], off[:, b:b + 1], ALU.add,
                                           ALU.add))
                chain(V.copy_predicated(fb[:, 3, :], fb[:, 2, :].bitcast(I32), fb[:, 4, :]))
            slot_places(fb[:, 3, :], fb[:, 5, :], fb[:, 6, :], fb[:, 7, :])
            for n in range(NT):
                if n >= 4:
                    dve.wait_ge(f_used, n - 3)
                V.tensor_scalar(fsc[:, n % 4, :], iota_f[:, 0:FT], fb[:, 5, n:n + 1], None, ALU.is_equal)
                V.tensor_scalar(fsa[:, n % 4, :], iota_f[:, 0:P], fb[:, 6, n:n + 1], node1f[:, n:n + 1],
                                ALU.is_equal, ALU.mult).then_inc(f_code, 1)
            dve.wait_ge(f_used, NT)
            chain(V.tensor_scalar(fd[:, 0, :], pm[0][:, 0:FT], -1.0, None, ALU.add))
            V.tensor_scalar(fgi[:, :], fd[:, 0, :], 0.0, None, ALU.max)
            chain(V.tensor_scalar(fd[:, 1, :], fd[:, 0, :], 0.0, float(2 ** 20), ALU.is_lt, ALU.mult))
            V.tensor_tensor(fsi[:, :], fd[:, 1, :], fd[:, 0, :], ALU.add).then_inc(f_idx, 1)

            def f_sum(i, u, reused):
                    t = 4 * i + u
                    kb = dve.value_load(fbin[0:1, bass.ds(t, 1)], min_val=0, max_val=K_BINS - 1)
                    dve.wait_ge(f_mm, t + 1)
                    if reused:
                        dve.wait_ge(f_out[u], 16 * i)
                    V.scalar_tensor_tensor(out=fout[:, u, :], in0=ag[u % 2][:, :],
                                           scalar=exf[:, 7, bass.ds(kb, 1)].bitcast(F32),
                                           in1=frow[:, u, 2 * D:4 * D].bitcast(F32), op0=ALU.mult,
                                           op1=ALU.add).then_inc(f_add, 1)

            for u in range(4):
                f_sum(0, u, False)
            with dve.Fori(1, FT // 4) as i:
                for u in range(4):
                    f_sum(i, u, True)


_INS = ['x', 'src', 'dst', 'edge_type_8', 'L0_gnn_W_self', 'L0_gnn_b_self', 'L0_gnn_W_rel', 'L0_gnn_b_rel', 'L0_ffn_W']


def kernel(**inputs):
    import numpy as _np
    import concourse.bacc as _bacc
    from concourse import mybir as _mybir
    from concourse.bass_utils import run_bass_kernel_spmd as _run

    nc = _bacc.Bacc("TRN2", target_bir_lowering=False, num_devices=1)
    arrays, args = {}, []
    for name in _INS:
        a = _np.ascontiguousarray(inputs[name])
        arrays[f"in_{name}"] = a
        args.append(nc.dram_tensor(f"in_{name}", a.shape, _mybir.dt.from_np(a.dtype), kind="ExternalInput").ap())
    out = nc.dram_tensor("out_0", (N, D), _mybir.dt.float32, kind="ExternalOutput").ap()
    build(nc, *args, out)
    r = _run(nc, [arrays], core_ids=[0])
    return r.results[0]["out_0"]
```

```python
import concourse.bass as bass
from concourse import mybir
from contextlib import ExitStack

F32 = mybir.dt.float32
F16 = mybir.dt.float16
I32 = mybir.dt.int32
ALU = mybir.AluOpType
ACT = mybir.ActivationFunctionType
AX_X = mybir.AxisListType.X

P = 128
N = 2500
D = 512
DK = D // P
NT = -(-N // P)
NPAD = NT * P
LAST = N - (NT - 1) * P
R = 8
NW = 2 * R + 1
SELF = NW - 1
E = 80000
EC = E // P
STEPS = 4
ITS = NT // STEPS
ECP = 642
GT = 2
BLOCKS = [[(0, 350, 388), (350, 275, 314)], [(0, 300, 338), (300, 325, 364)]]
BC = 350
WIN = 388
PERMS = [(0, 0, 0, 35, (4, 3, 3), 388), (0, 350, 35, 20, (5, 5, 4), 314), (1, 0, 55, 20, (5, 5, 5), 338),
         (1, 300, 75, 18, (5, 5, 5, 4), 364)]
SLOTS = 10
SELF_ITS = NT // 2
PERM_SUMS = PERMS[3][3] - SELF_ITS
LTD = 702
LT = 18
LIT = LTD // LT
VROWS = R * NPAD
K_BINS = 8
FT = 28
BINS = [-1.5, -1.0, -0.5, 0.0, 0.5, 1.0, 1.5]
RND = 12582912.0
YS = 512.0
FAR = -20000.0
assert EC * P == E and STEPS * ITS == NT and LIT * LT == LTD and LIT < R * ITS
for blocks in BLOCKS:
    assert sum(w for _, _, w in blocks) == LTD and blocks[-1][0] + blocks[-1][1] >= EC
    assert all((min(c0 + n, EC) - c0) * P + NT * (GT * P - 1) < (w + GT) * P for c0, n, w in blocks)
for d, c0, n0, its, cols, win in PERMS:
    end = c0 + its * sum(cols)
    assert end == BLOCKS[d][1][0] or EC <= end <= ECP
assert N + K_BINS * (P - 1) < (FT + 1) * P
CHUNK_A = LT // 2
PER_STEP = [range(0, 4), range(4, 8), range(8, 12), range(12, 18)]


def perm_step(perm, n, u):
    at = PERMS.index(perm)
    return sum(its * len(cols) for _, _, _, its, cols, _ in PERMS[:at]) + len(perm[4]) * (n - perm[2]) + u


def perm_column(perm, n, u, v):
    return perm[1] + sum(perm[4]) * (n - perm[2]) + sum(perm[4][:u]) + v


def build(nc, x, src, dst, etype, w_self, b_self, w_rel, b_rel, w_ffn, out):
    ctx = ExitStack()
    with ctx:
        def sb(name, shape, dt):
            return ctx.enter_context(nc.sbuf_tensor(name, shape, dt))

        def sem(name):
            return ctx.enter_context(nc.semaphore(name))

        table = [nc.dram_tensor(f"table{d}", (VROWS, 2 * D), F16) for d in range(2)]
        rows = nc.dram_tensor("ffn_rows", (NPAD, 2 * D), I32)

        big = sb("big", [P, 36864], F16)
        yT = big[:, 0:2 * DK * NPAD].rearrange("p (h k n) -> p h k n", h=2, k=DK)
        wmov = big[:, 20480:28672].rearrange("p (b h k n) -> p b h k n", b=2, h=2, k=DK)
        wraw = [big[:, 20480 + 4096 * s:20480 + 4096 * (s + 1)].bitcast(F32) for s in range(4)]
        wf = big[:, 0:32768]
        wfraw = wraw[3]
        acc = sb("acc", [P, NT * D], F32)
        gath = sb("gath", [P, LT * 2 * D], F16)
        gf = gath[:, :].bitcast(F32)
        ytmp = gf[:, 0:4 * D].rearrange("p (s n) -> p s n", s=4)
        e0 = 4 * D
        ea = [gf[:, e0 + ECP * i:e0 + ECP * (i + 1)] for i in range(5)]
        e_src, e_dst, e_type = (a.bitcast(I32) for a in ea[0:3])
        e_bin, e_pos = ea[3], ea[4]
        b0 = e0 + 5 * ECP
        e_tmp = [gf[:, b0 + D + D // 2 + ECP * i:b0 + D + D // 2 + ECP * (i + 1)].bitcast(I32) for i in range(2)]
        braw = gf[0:NW, b0:b0 + D]
        frow = gath[:, 0:4 * 4 * D].rearrange("p (s n) -> p s n", s=4)
        fyT = gath[:, 8192:8192 + 2 * 2 * D].rearrange("p (s n) -> p s n", s=2)
        fout = gath[:, 10240:10240 + 4096].bitcast(F32).rearrange("p (s n) -> p s n", s=4)
        xin = gath[:, 8192:12288].bitcast(F32).rearrange("p (s n) -> p s n", s=4)
        ftmp = gath[:, 12288:16384].bitcast(F32).rearrange("p (s n) -> p s n", s=4)

        trow = sb("trow", [P, 4, 2 * D], F16)
        wstage = sb("wstage", [P, DK, P], F32)
        bias = sb("bias", [P, 2, D], F32)
        code_hi0, code_lo0 = sb("code_hi0", [P, ECP], F32), sb("code_lo0", [P, ECP], F32)
        c1 = 28672
        e_hi = [code_hi0[:, :], big[:, c1:c1 + 2 * ECP].bitcast(F32)]
        e_lo = [code_lo0[:, :], big[:, c1 + 2 * ECP:c1 + 4 * ECP].bitcast(F32)]
        e_row = [big[:, c:c + ECP] for c in (32768, c1 + 4 * ECP)]
        e_col = [big[:, c:c + ECP] for c in (32768 + ECP, c1 + 5 * ECP)]
        work = sb("work", [P, 2, WIN], F32)
        ind, scan = work[:, 0, 0:BC], work[:, 1, 0:BC]
        zeros = sb("zeros", [P, BC], F16)
        ohc = sb("ohc", [P, SLOTS, WIN], F16)
        ohr = sb("ohr", [P, SLOTS, 2, P], F16)
        loc = sb("loc", [P, 2 * LTD + 4], F16)
        gidx = sb("gidx", [P, 2 * LTD], I32)
        gidr = sb("gidr", [P, LT], I32)
        oh = sb("oh", [P, LT, P], F16)
        lbin = sb("lbin", [1, 2 * LTD // GT], I32)
        iota_i = work[:, 0, :].bitcast(I32)
        tbc, ge = work[0:32, 0, 0:P], work[0:32, 1, :]
        iota_f = sb("iota_f", [P, WIN // GT], F32)
        iota_h = sb("iota_h", [P, WIN], F16)
        dif = sb("dif", [P, P], I32)
        ident = sb("ident", [P, P], F32)
        ident_h = sb("ident_h", [P, P], F16)
        before = sb("before", [P, P], F32)
        ones = sb("ones", [P, P], F32)
        node1 = sb("node1", [P, NT], I32)
        node1f = sb("node1f", [P, NT], F32)
        invalid = sb("invalid", [P, NT], F32)
        ssq = sb("ssq", [P, NW + 1], F32)
        ssum = sb("ssum", [P, 1], F32)
        ex = sb("ex", [P, 12], I32)
        exf = sb("exf", [P, 12, K_BINS], I32)
        ssf = sb("ssf", [P, K_BINS], F32)
        st = sb("st", [P, NT, 6], F32)
        mv = sb("mv", [P, NT, 2], F32)
        ln = sb("ln", [P, 6, NT], F32)
        cnt = sb("cnt", [P, 2 * NT], F32)
        pre = sb("pre", [P, 2 * NT], F32)
        off = sb("off", [P, 2 * NT], F32)
        tcol = sb("tcol", [32, 4], F32)
        late = wstage[:, :, :].rearrange("p c n -> p (c n)")
        fb = late[:, 0:8 * NT].rearrange("p (a n) -> p a n", a=8)
        fd = late[:, 8 * NT:8 * NT + 4 * FT].rearrange("p (a n) -> p a n", a=4)
        fgi = sb("fgi", [P, FT], I32)
        fsi = sb("fsi", [P, FT], I32)
        fbin = sb("fbin", [1, FT], I32)
        ohrf = ohr[:, :, :, :].rearrange("p s h n -> p (s h n)").bitcast(F32)
        fsa = ohrf[:, 0:4 * P].rearrange("p (s n) -> p s n", s=4)
        fsc = ohrf[:, 4 * P:4 * (P + FT)].rearrange("p (s n) -> p s n", s=4)

        bank = [ctx.enter_context(nc.psum_tensor(f"bank{i}", [P, D], F32)) for i in range(8)]
        pj = bank[0:2]
        wt = bank[2]
        pm = bank[3:5]
        ag = bank[5:8]

        ld_x = [sem(f"ld_x{i}") for i in range(ITS)]
        ld_edges = sem("ld_edges")
        ld_b = sem("ld_b")
        ld_bias = [sem(f"ld_bias{i}") for i in range(2)]
        banks_set = sem("banks_set")
        bias_in = sem("bias_in")
        ld_sq = [sem(f"ld_sq{i}") for i in range(4)]
        ld_wc = sem("ld_wc")
        ld_wf = sem("ld_wf")
        ld_x2 = [sem(f"ld_x2{i}") for i in range(4)]
        consts_i = sem("consts_i")
        consts = sem("consts")
        pads = sem("pads")
        squares = sem("squares")
        step = sem("step")
        root = sem("root")
        small_in = sem("small_in")
        small_out = sem("small_out")
        y_ready = sem("y_ready")
        yt_mm = sem("yt_mm")
        yt_hi = sem("yt_hi")
        yt_lo = sem("yt_lo")
        wt_mm = sem("wt_mm")
        wt_hi = sem("wt_hi")
        wt_lo = sem("wt_lo")
        proj = sem("proj")
        proj_hi = sem("proj_hi")
        proj_read = sem("proj_read")
        row_out = [sem(f"row_out{i}") for i in range(4)]
        rank = sem("rank")
        hot_ready = sem("hot_ready")
        code_ready = sem("code_ready")
        code_used = sem("code_used")
        perm_done = sem("perm_done")
        lists = sem("lists")
        oh_ready = sem("oh_ready")
        agg = sem("agg")
        agg_read = sem("agg_read")
        acc_zero = sem("acc_zero")
        got = [sem(f"got{i}") for i in range(LT)]
        idx_copied = sem("idx_copied")
        wf_sq = sem("wf_sq")
        wf_hi = sem("wf_hi")
        wf_lo = sem("wf_lo")
        x1_done = sem("x1_done")
        f_norm = sem("f_norm")
        f_hi = sem("f_hi")
        f_lo = sem("f_lo")
        f_rows = [sem(f"f_rows{i}") for i in range(4)]
        f_x1 = sem("f_x1")
        f_code = sem("f_code")
        f_used = sem("f_used")
        f_perm = sem("f_perm")
        f_idx = sem("f_idx")
        f_got = [sem(f"f_got{i}") for i in range(4)]
        f_tr = sem("f_tr")
        f_yT = sem("f_yT")
        f_mm = sem("f_mm")
        f_add = sem("f_add")
        f_out = [sem(f"f_out{i}") for i in range(4)]

        block = ctx.enter_context(nc.Block())
        w_order = list(range(1, NW)) + [0]

        def w_dram(w):
            return w_self if w == SELF else w_rel[w]

        @block.sync
        def _(sp):
            xg = x[0:(NT - 1) * P, :].rearrange("(t p) d -> p t d", p=P)
            accv = acc[:, :].rearrange("p (t d) -> p t d", t=NT)
            sp.wait_ge(pads, 1)
            for tile, edges in ((e_src, src), (e_dst, dst), (e_type, etype)):
                sp.dma_start(tile[:, 0:EC], edges.rearrange("(p f) -> p f", p=P)).then_inc(ld_edges, 16)
            for g in range(ITS):
                hi = min(STEPS * (g + 1), NT - 1)
                sp.dma_start(accv[:, STEPS * g:hi, :], xg[:, STEPS * g:hi, :]).then_inc(ld_x[g], 16)
            sp.wait_ge(pads, 2)
            sp.dma_start(accv[0:LAST, NT - 1, :], x[(NT - 1) * P:N, :]).then_inc(ld_x[ITS - 1], 16)
            for i, w in enumerate(w_order):
                if i >= 4:
                    sp.wait_ge(squares, i - 3)
                sp.dma_start(wraw[(i + 2) % 4].rearrange("p (c d) -> p c d", c=DK),
                             w_dram(w).rearrange("(c p) d -> p c d", p=P)).then_inc(ld_sq[(i + 2) % 4], 16)
                if i == 3:
                    sp.wait_ge(pads, 3)
                    sp.dma_start(braw[SELF:NW, :], b_self.rearrange("(a d) -> a d", a=1)).then_inc(ld_b, 16)
                    sp.dma_start(braw[0:SELF, :], b_rel).then_inc(ld_b, 16)
                    for w in range(2):
                        sp.dma_start(bias[:, w, :], b_rel[w:w + 1, :].broadcast_to([P, D])).then_inc(ld_bias[w], 16)

            def w_chunk(w, q, own=None):
                sp.wait_ge(wt_mm, 4 * w + q + 4)
                source = w_rel[bass.ds(w + 1, 1), :, bass.ds(q * P, P)].rearrange(
                    "a (c p) d -> p (a c) d", p=P) if own is None else \
                    own[:, bass.ds(q * P, P)].rearrange("(c p) d -> p c d", p=P)
                sp.dma_start(wstage[:, :, :], source).then_inc(ld_wc, 16)

            def store_rows(w, q, u, d, r):
                sp.wait_ge(proj_read, NT * w + STEPS * q + u + 3)
                sp.dma_start(table[d].ap()[bass.ds((r * NT + STEPS * q + u) * P, P), :],
                             trow[:, u, :]).then_inc(row_out[u], 16)

            def relation(w, d, own=None):
                with sp.Fori(0, DK) as q:
                    w_chunk(w, q, own)
                    for u in range(STEPS):
                        store_rows(w, q, u, d, w - R * d)
                for u in range(STEPS):
                    store_rows(w, DK, u, d, w - R * d)

            def load_bias(w, buf, source):
                sp.wait_ge(bias_in, NT * (w - 1))
                sp.dma_start(bias[:, buf, :], source.broadcast_to([P, D])).then_inc(ld_bias[buf], 16)

            relation(0, 0)
            with sp.Fori(0, R // 2 - 1) as pair:
                for par in range(2):
                    w = 2 * pair + par + 1
                    load_bias(w + 1, par, b_rel[bass.ds(w + 1, 1), :])
                    relation(w, 0)
            load_bias(R, 0, b_rel[R:R + 1, :])
            relation(R - 1, 0)
            with sp.Fori(R // 2, R - 1) as pair:
                for par in range(2):
                    w = 2 * pair + par
                    load_bias(w + 1, 1 - par, b_rel[bass.ds(w + 1, 1), :])
                    relation(w, 1)
            load_bias(2 * R - 1, 1, b_rel[2 * R - 1:2 * R, :])
            relation(2 * R - 2, 1)
            load_bias(SELF, 0, b_self.rearrange("(a d) -> a d", a=1))
            relation(2 * R - 1, 1, w_self)

            for k in range(K_BINS):
                if k == 0:
                    sp.wait_ge(proj_read, NT * NW + 2)
                else:
                    sp.wait_ge(wf_lo, k)
                sp.dma_start(wfraw.rearrange("p (c o) -> p c o", c=DK),
                             w_ffn[k].rearrange("(c p) o -> p c o", p=P)).then_inc(ld_wf, 16)

            sp.wait_ge(agg, 2 * LTD + LT)

            def load_x(j, u, n=P):
                sp.dma_start(xin[0:n, u, :], x[bass.ds(j * P, n), :]).then_inc(ld_x2[u], 16)

            for u in range(STEPS):
                load_x(u, u)
            with sp.Fori(1, ITS - 1) as i:
                for u in range(STEPS):
                    sp.wait_ge(x1_done, STEPS * i + u - STEPS + 1)
                    load_x(STEPS * i + u, u)
            for u in range(STEPS):
                j = NT - STEPS + u
                sp.wait_ge(x1_done, j - STEPS + 1)
                load_x(j, u, P if j < NT - 1 else LAST)

            with sp.Fori(0, NT) as j:
                sp.wait_ge(x1_done, j + 1)
                sp.dma_start(rows.ap()[bass.ds(j * P, P), D:2 * D],
                             acc[:, bass.ds(j * D, D)].bitcast(I32)).then_inc(f_x1, 16)
            with sp.Fori(0, ITS) as i:
                for u in range(STEPS):
                    j = STEPS * i + u
                    sp.wait_ge(f_lo, j + 1)
                    sp.dma_start(rows.ap()[bass.ds(j * P, P), 0:D], trow[:, u, :].bitcast(I32)).then_inc(f_rows[u], 16)

        @block.gpsimd
        def _(pool):
            nc.gpsimd.iota(iota_i[:, :], pattern=[[1, WIN]], base=0, channel_multiplier=0)
            nc.gpsimd.iota(dif[:, :], pattern=[[1, P]], base=0, channel_multiplier=-1)
            nc.gpsimd.iota(node1[:, :], pattern=[[P, NT]], base=1, channel_multiplier=1).then_inc(consts_i, 1)

            pool.wait_ge(y_ready, NT)
            nc.gpsimd.memset(acc[:, :], 0.0).then_inc(acc_zero, 1)

            def gather_set(i, d, which):
                v0, v1 = (0, CHUNK_A) if which == 0 else (CHUNK_A, LT)
                pool.wait_ge(agg, LT * i + v1)
                nc.gpsimd.tensor_copy(gidr[:, v0:v1], gidx[:, bass.ds(LT * i + v0, v1 - v0)]).then_inc(idx_copied, 1)
                pool.wait_ge(idx_copied, 2 * i + which + 1)
                pool.nop(nofuse=True)
                for v in range(v0, v1):
                    pool.indirect_dma_start(
                        out=gath[:, v * 2 * D:(v + 1) * 2 * D], out_offset=None, in_=table[d].ap(),
                        in_offset=bass.IndirectOffsetOnAxis(ap=gidr[:, v:v + 1], axis=0)).then_inc(got[v], 16)

            for d in range(2):
                pool.wait_ge(lists, 2 * d + 1)
                for u in range(4):
                    pool.wait_ge(row_out[u], 16 * (1 + R * ITS * (d + 1)))
                begin, full = LIT * d, BLOCKS[d][0][2] // LT
                with pool.Fori(begin, begin + full) as i:
                    for which in range(2):
                        gather_set(i, d, which)
                pool.wait_ge(lists, 2 * d + 2)
                with pool.Fori(begin + full, begin + LIT) as i:
                    for which in range(2):
                        gather_set(i, d, which)

            with pool.Fori(0, ITS) as i:
                for u in range(STEPS):
                    pool.wait_ge(f_hi, STEPS * i + u + 1)
                    nc.gpsimd.tensor_tensor(trow[:, u, D:2 * D], ftmp[:, u, :], trow[:, u, 0:D],
                                            ALU.subtract).then_inc(f_lo, 1)

            pool.wait_ge(f_idx, 1)
            for u in range(4):
                pool.wait_ge(f_rows[u], 16 * ITS)
            pool.wait_ge(f_x1, 16 * NT)

            def fetch(t):
                pool.indirect_dma_start(out=frow[:, t % 4, :].bitcast(I32), out_offset=None, in_=rows.ap(),
                                        in_offset=bass.IndirectOffsetOnAxis(ap=fgi[:, t:t + 1], axis=0)
                                        ).then_inc(f_got[t % 4], 16)

            def send(t):
                pool.wait_ge(f_add, t + 3)
                pool.indirect_dma_start(out=out, out_offset=bass.IndirectOffsetOnAxis(ap=fsi[:, t:t + 1], axis=0),
                                        in_=fout[:, t % 4, :], in_offset=None,
                                        bounds_check=N - 1, oob_is_err=False).then_inc(f_out[t % 4], 16)

            for t in range(4):
                fetch(t)
            for t in range(FT):
                send(t)
                if t + 4 < FT:
                    fetch(t + 4)
            for u in range(4):
                pool.wait_ge(f_out[u], 16 * (FT // 4))

        @block.scalar
        def _(act):
            nc.scalar.sem_inc(agg_read, 3)
            nc.scalar.sem_inc(f_yT, 2)
            act.wait_ge(root, 1)
            nc.scalar.activation(ln[:, 1, :], ln[:, 0, :], ACT.Sqrt).then_inc(root, 1)
            for i, w in enumerate(w_order):
                act.wait_ge(ld_sq[(i + 2) % 4], 16 * (i // 4 + 1))
                if i == 0:
                    act.wait_ge(pads, 3)
                if i:
                    act.wait_ge(squares, i)
                nc.scalar.activation(trow[:, 0:2, :].rearrange("p s n -> p (s n)"), wraw[(i + 2) % 4], ACT.Square,
                                     accum_out=ssq[:, w:w + 1]).then_inc(squares, 1)
                for n in range(2 * i, min(2 * i + 2, NT)):
                    act.wait_ge(yt_mm, n + 1)
                    nc.scalar.copy(yT[:, 0, :, n * P:(n + 1) * P],
                                   pj[n % 2][:, :].rearrange("p (k n) -> p k n", k=DK)).then_inc(yt_hi, 1)
            act.wait_ge(ld_b, 32)
            nc.scalar.activation(trow[0:NW, 2, 0:D], braw, ACT.Square, scale=1.0 / 32,
                                 accum_out=ssq[0:NW, NW:NW + 1]).then_inc(squares, 1)

            def w_high(buf, c, q):
                act.wait_ge(wt_mm, c + 1)
                nc.scalar.activation(wmov[:, buf, 0, q, :] if isinstance(q, int) else
                                     wmov[:, buf, 0].rearrange("p k n -> p (k n)")[:, bass.ds(q * D, D)],
                                     wt[:, :], ACT.Copy, scale=ex[:, 3:4].bitcast(F32)).then_inc(wt_hi, 1)

            act.wait_ge(small_in, 7)
            for q in range(DK):
                w_high(0, q, q)
            act.wait_ge(squares, NW + 1)

            def put_bias(w, j, slot, buf):
                act.wait_ge(proj_read, NT * w + j + 1)
                nc.scalar.activation(pj[slot][:, :], bias[:, buf, :], ACT.Copy,
                                     scale=ex[:, 11:12].bitcast(F32)).then_inc(bias_in, 1)

            act.wait_ge(banks_set, 1)
            act.wait_ge(ld_bias[0], 16)
            for slot in range(2):
                put_bias(0, slot, slot, 0)

            def row_high(w, q, u):
                act.wait_ge(proj, NT * w + STEPS * q + u + 1)
                act.wait_ge(row_out[u], 16 * (ITS * w + q + 1))
                nc.scalar.activation(trow[:, u, 0:D], pj[u % 2][:, :], ACT.Copy,
                                     scale=2.0 ** -14).then_inc(proj_hi, 1)

            def multiply_codes(n, u, perm):
                d, cols = perm[0], perm[4]
                act.wait_ge(hot_ready, perm_step(perm, n, u) + 1)
                act.nop(nofuse=True)
                for v in range(cols[u]):
                    s = (u % 2) * 5 + v
                    f = perm_column(perm, n, u, v)
                    nc.scalar.activation(ohr[:, s, 1, :], ohr[:, s, 0, :], ACT.Copy, scale=e_lo[d][:, bass.ds(f, 1)])
                    last = nc.scalar.activation(ohr[:, s, 0, :], ohr[:, s, 0, :], ACT.Copy,
                                                scale=e_hi[d][:, bass.ds(f, 1)])
                last.then_inc(code_ready, 1)

            def iteration(w, nxt, q, perm, chunk):
                for u in range(STEPS):
                    row_high(w, q, u)
                    if u == 2 and chunk:
                        w_high(nxt, 4 * (w + 1) + q, q)
                    if perm and u < len(perm[4]):
                        multiply_codes(ITS * (w - 1) + q, u, perm)
                    if chunk or u < 2:
                        put_bias(w, STEPS * q + u + 2, u % 2, 1 - nxt)
                    else:
                        if u == 2:
                            act.wait_ge(ld_bias[nxt], 8 * w + (16 if nxt else 24))
                        put_bias(w + 1, u - 2, u % 2, nxt)

            def relation(w, nxt, perm):
                with act.Fori(0, DK) as q:
                    iteration(w, nxt, q, perm, True)
                iteration(w, nxt, DK, perm, False)

            relation(0, 1, None)
            with act.Fori(0, 3) as pair:
                for par in range(2):
                    relation(2 * pair + par + 1, par, PERMS[0])
            relation(7, 0, PERMS[0])
            for perm, first in ((PERMS[1], 8), (PERMS[2], 12)):
                with act.Fori(0, 2) as pair:
                    for par in range(2):
                        relation(2 * pair + par + first, 1 - par, perm)
            with act.Fori(0, SELF_ITS - 1) as i:
                for u in range(STEPS):
                    multiply_codes(PERMS[3][2] + i, u, PERMS[3])
                    if u % 2 == 0:
                        put_bias(SELF, 2 * i + u // 2 + 2, u // 2, 0)
            with act.Fori(PERMS[3][2] + SELF_ITS - 1, PERMS[3][2] + PERMS[3][3]) as n:
                for u in range(STEPS):
                    multiply_codes(n, u, PERMS[3])

            for u in range(4):
                act.wait_ge(row_out[u], 16 * (1 + 2 * R * ITS))
            for k in range(K_BINS):
                act.wait_ge(ld_wf, 16 * (k + 1))
                if k:
                    act.wait_ge(wf_sq, k)
                nc.scalar.activation(trow[:, 0:2, :].rearrange("p s n -> p (s n)"), wfraw, ACT.Square,
                                     accum_out=ssf[:, k:k + 1]).then_inc(wf_sq, 1)
                act.wait_ge(small_in, 13 + k)
                nc.scalar.activation(wf[:, 4096 * k:4096 * k + 2048], wfraw, ACT.Copy,
                                     scale=exf[:, 3, k:k + 1].bitcast(F32)).then_inc(wf_hi, 1)

            act.wait_ge(wf_sq, K_BINS)
            act.wait_ge(root, 3)
            nc.scalar.activation(ln[:, 1, :], ln[:, 0, :], ACT.Sqrt).then_inc(root, 1)
            act.wait_ge(f_norm, 1)

            def norm_high(i, u, reused):
                j = STEPS * i + u
                row = acc[:, bass.ds(j * D, D)]
                scale, shift = ln[:, 5, bass.ds(j, 1)], ln[:, 2, bass.ds(j, 1)]
                if reused:
                    act.wait_ge(f_lo, j - STEPS + 1)
                    act.wait_ge(f_rows[u], 16 * i)
                    act.nop(nofuse=True)
                nc.scalar.activation(ftmp[:, u, :], row, ACT.Identity, bias=shift, scale=scale)
                nc.scalar.activation(trow[:, u, 0:D], row, ACT.Identity, bias=shift, scale=scale).then_inc(f_hi, 1)

            for u in range(STEPS):
                norm_high(0, u, False)
            with act.Fori(1, ITS) as i:
                for u in range(STEPS):
                    norm_high(i, u, True)

            with act.Fori(0, FT // 4) as i:
                for u in range(4):
                    act.wait_ge(f_tr, 4 * i + u + 1)
                    nc.scalar.copy(fyT[:, u % 2, :], pj[u % 2][:, :].bitcast(F16)).then_inc(f_yT, 1)

        @block.tensor
        def _(pe):
            nc.tensor.sem_inc(code_used, 2)
            nc.tensor.sem_inc(agg, LT)

            pe.wait_ge(consts, 1)

            def small(outp, lhsT, rhs):
                return nc.tensor.matmul(outp, lhsT, rhs, start=True, stop=True)


            def offsets(base, n_bins=NT, wins=None, d=0):
                wins = wins or [w // GT for _, _, w in BLOCKS[d]]
                blocks = len(wins)
                pe.wait_ge(small_in, base)
                small(ag[0][:, 0:blocks * n_bins], before[:, :], cnt[:, 0:blocks * n_bins])
                for b in range(blocks):
                    mm = small(ag[1][0:n_bins, b:b + 1], cnt[:, b * n_bins:(b + 1) * n_bins], ones[:, 0:1])
                mm.then_inc(small_out, 1)
                for b in range(blocks):
                    pe.wait_ge(small_in, base + 1 + 2 * b)
                    small(ag[0][:, 0:n_bins], tbc[0:n_bins, :], before[0:n_bins, 0:n_bins])
                    small(ag[1][0:n_bins, 0:1], before[0:n_bins, 0:n_bins], tcol[0:n_bins, b:b + 1]
                          ).then_inc(small_out, 1)
                    pe.wait_ge(small_in, base + 2 + 2 * b)
                    small(ag[2][0:1, 0:wins[b]], ones[0:n_bins, 0:1], ge[0:n_bins, 0:wins[b]]).then_inc(small_out, 1)

            with pe.Fori(0, NT // 4) as i:
                for u in range(4):
                    pe.wait_ge(y_ready, 4 * i + u + 1)
                    pe.wait_ge(yt_lo, 4 * i + u + 1)
                    for k in range(DK):
                        mm = nc.tensor.transpose(pj[u % 2][:, k * P:(k + 1) * P], ytmp[:, u, k * P:(k + 1) * P],
                                                 ident[:, :])
                    mm.then_inc(yt_mm, 1)

            offsets(1)

            pe.wait_ge(yt_lo, NT + 2)
            for slot in range(2):
                mm = nc.tensor.matmul(pj[slot][:, :], zeros[:, 0:P], big[:, 0:D], start=True, stop=True)
            mm.then_inc(banks_set, 1)

            pe.wait_ge(small_in, 6)
            small(ag[0][:, 0:1], ones[:, :], ssum[:, :]).then_inc(small_out, 1)

            def w_transpose(c, raw):
                pe.wait_ge(wt_lo, c + 1)
                for oc in range(DK):
                    mm = nc.tensor.transpose(wt[:, oc * P:(oc + 1) * P], raw[oc], ident[:, :])
                mm.then_inc(wt_mm, 1)

            pe.wait_ge(ld_sq[(NW - 1 + 2) % 4], 16 * ((NW - 1) // 4 + 1))
            raw0 = wraw[(NW - 1 + 2) % 4]
            for q in range(DK):
                w_transpose(q, [raw0[:, oc * D + q * P:oc * D + (q + 1) * P] for oc in range(DK)])
            stage = [wstage[:, oc, :] for oc in range(DK)]

            def project(w, buf, j, slot):
                pe.wait_ge(bias_in, NT * w + j + 1)
                pe.nop(nofuse=True)
                ps = pj[slot][:, :]
                for k in range(DK):
                    yh = big[:, bass.ds(k * NPAD + j * P, P)]
                    yl = big[:, bass.ds((DK + k) * NPAD + j * P, P)]
                    nc.tensor.matmul(ps, yh, wmov[:, buf, 0, k, :], start=False, stop=False, skip_group_check=True)
                    nc.tensor.matmul(ps, yh, wmov[:, buf, 1, k, :], start=False, stop=False, skip_group_check=True)
                    mm = nc.tensor.matmul(ps, yl, wmov[:, buf, 0, k, :], start=False, stop=(k == DK - 1),
                                          skip_group_check=True)
                mm.then_inc(proj, 1)

            def permute(n, u, perm):
                cols, win = perm[4:6]
                pe.wait_ge(code_ready, perm_step(perm, n, u) + 1)
                for v in range(cols[u]):
                    s = (u % 2) * 5 + v
                    for h in range(2):
                        mm = nc.tensor.matmul(pm[h][:, 0:win], ohr[:, s, h, :], ohc[:, s, 0:win], start=False,
                                              stop=False, skip_group_check=True)
                mm.then_inc(code_used, 1)

            def open_block(n, win):
                if n:
                    pe.wait_ge(lists, n)
                for h in range(2):
                    nc.tensor.matmul(pm[h][:, 0:win], zeros[:, 0:P], iota_h[:, 0:win], start=True,
                                     stop=False, skip_group_check=True)

            def close_block(win):
                for h in range(2):
                    mm = nc.tensor.matmul(pm[h][:, 0:win], zeros[:, 0:P], iota_h[:, 0:win], start=False,
                                          stop=True, skip_group_check=True)
                mm.then_inc(perm_done, 1)

            def sum_tiles(i, vs):
                for v in vs:
                    t = LT * i + v
                    ps = ag[v // GT % 3][:, :]
                    if v % GT == 0:
                        pe.wait_ge(oh_ready, t + GT)
                        pe.wait_ge(agg_read, LT // GT * i + v // GT + 1)
                    pe.wait_ge(got[v], 16 * (i + 1))
                    nc.tensor.matmul(ps, oh[:, v, :], gath[:, v * 2 * D:v * 2 * D + D], start=(v % GT == 0),
                                     stop=False)
                    nc.tensor.matmul(ps, oh[:, v, :], gath[:, v * 2 * D + D:(v + 1) * 2 * D], start=False,
                                     stop=(v % GT == GT - 1)).then_inc(agg, 1)

            def iteration(w, buf, q, chunk, perm, summing):
                for u in range(STEPS):
                    project(w, buf, STEPS * q + u, u % 2)
                    if u == 2 and chunk:
                        pe.wait_ge(ld_wc, 16 * (4 * w + q + 1))
                        w_transpose(4 * (w + 1) + q, stage)
                    if summing is not None:
                        sum_tiles(summing, PER_STEP[u])
                    if perm and u:
                        permute(ITS * (w - 1) + q, u - 1, perm)

            def relation(w, par, perm=None, summing=False, lead=0):
                pe.wait_ge(wt_lo, 4 * (w + 1) + 1)
                pe.nop(nofuse=True)
                at = ITS * (w - R) - 1 if summing else None
                for q in range(lead):
                    iteration(w, par, q, True, perm, None)
                with pe.Fori(lead, DK) as q:
                    iteration(w, par, q, True, perm, at + q if summing else None)
                iteration(w, par, DK, False, perm, at + DK if summing else None)

            pe.wait_ge(yt_lo, NT + 2)
            relation(0, 0)
            open_block(0, BLOCKS[0][0][2])
            with pe.Fori(0, 2) as pair:
                for par in range(2):
                    relation(2 * pair + par + 1, 1 - par, PERMS[0])
            relation(5, 1, PERMS[0])
            offsets(8, d=1)
            for w in range(6, 8):
                relation(w, w % 2, PERMS[0])
            close_block(BLOCKS[0][0][2])
            open_block(1, BLOCKS[0][1][2])
            relation(8, 0, PERMS[1], True, lead=1)
            for w in range(9, 12):
                relation(w, w % 2, PERMS[1], True)
            close_block(BLOCKS[0][1][2])
            open_block(2, BLOCKS[1][0][2])
            with pe.Fori(0, 2) as pair:
                for par in range(2):
                    relation(2 * pair + par + 12, par, PERMS[2], True)
            close_block(BLOCKS[1][0][2])
            open_block(3, BLOCKS[1][1][2])

            pe.wait_ge(wt_lo, 4 * NW + 1)
            def permute_last(n, u):
                permute(n - (u == 0), (u - 1) % STEPS, PERMS[3])

            for u in range(STEPS):
                if u % 2 == 0:
                    project(SELF, 0, u // 2, u // 2)
                if u:
                    permute_last(PERMS[3][2], u)
            with pe.Fori(1, SELF_ITS) as q:
                for u in range(STEPS):
                    if u % 2 == 0:
                        project(SELF, 0, 2 * q + u // 2, u // 2)
                    sum_tiles(LIT + q - 1, PER_STEP[u])
                    permute_last(PERMS[3][2] + q, u)
            with pe.Fori(0, PERM_SUMS) as i:
                for u in range(STEPS):
                    sum_tiles(LIT + (SELF_ITS - 1) + i, PER_STEP[u])
                    permute_last(PERMS[3][2] + SELF_ITS + i, u)
            permute_last(PERMS[3][2] + PERMS[3][3], 0)
            close_block(BLOCKS[1][1][2])
            rest = LIT + (SELF_ITS - 1) + PERM_SUMS
            with pe.Fori(0, K_BINS) as k:
                for half in range(2):
                    for vs in PER_STEP:
                        sum_tiles(rest + 2 * k + half, vs)
                    if half == 0:
                        pe.wait_ge(wf_sq, k + 1)
                        pe.wait_ge(small_in, 12 + k)
                        small(pj[0][:, 0:K_BINS], ones[:, :], ssf[:, :]).then_inc(small_out, 1)
            with pe.Fori(rest + 2 * K_BINS, 2 * LIT) as i:
                for vs in PER_STEP:
                    sum_tiles(i, vs)

            offsets(21, K_BINS, [FT])
            for n in range(NT):
                pe.wait_ge(f_code, n + 1)
                nc.tensor.matmul(pm[0][:, 0:FT], fsa[:, n % 4, :], fsc[:, n % 4, :], start=(n == 0),
                                 stop=(n == NT - 1)).then_inc(f_used, 1)

            def f_transpose(m, slot, uses):
                pe.wait_ge(f_got[slot], 16 * uses)
                pe.wait_ge(f_yT, m + 1)
                for c in range(2 * DK):
                    mm = nc.tensor.transpose(pj[slot % 2][:, :].bitcast(F16)[:, c * P:(c + 1) * P],
                                             frow[:, slot, c * P:(c + 1) * P], ident_h[:, :])
                mm.then_inc(f_tr, 1)

            def f_product(t, slot):
                pe.wait_ge(f_yT, t + 3)
                pe.wait_ge(f_add, t + 1)
                pe.nop(nofuse=True)
                kb = pe.value_load(fbin[0:1, bass.ds(t, 1)], min_val=0, max_val=K_BINS - 1)
                ps = ag[slot % 2][:, :]
                for k in range(DK):
                    wh = wf[:, bass.ds(kb * 4096 + k * D, D)]
                    wl = wf[:, bass.ds(kb * 4096 + 2048 + k * D, D)]
                    yh = fyT[:, slot % 2, k * P:(k + 1) * P]
                    yl = fyT[:, slot % 2, (DK + k) * P:(DK + k + 1) * P]
                    nc.tensor.matmul(ps, yh, wh, start=(k == 0), stop=False)
                    nc.tensor.matmul(ps, yh, wl, start=False, stop=False)
                    mm = nc.tensor.matmul(ps, yl, wh, start=False, stop=(k == DK - 1))
                mm.then_inc(f_mm, 1)

            pe.wait_ge(wf_lo, K_BINS)
            pe.wait_ge(f_idx, 1)
            f_transpose(0, 0, 1)
            with pe.Fori(0, FT // 4 - 1) as i:
                for u in range(4):
                    f_transpose(4 * i + u + 1, (u + 1) % 4, i + 1 + (u == 3))
                    f_product(4 * i + u, u)
            for u in range(4):
                t = FT - 4 + u
                if u < 3:
                    f_transpose(t + 1, u + 1, FT // 4)
                f_product(t, u)

        @block.vector
        def _(dve):
            V = nc.vector
            V.sem_inc(yt_lo, 2)
            V.sem_inc(wt_lo, 1)
            V.sem_inc(proj_read, 2)
            V.sem_inc(f_add, 2)
            for u in range(4):
                V.sem_inc(row_out[u], 16)
            steps = [0]

            def chain(ins):
                steps[0] += 1
                ins.then_inc(step, 1)
                dve.wait_ge(step, steps[0])

            V.memset(e_src[:, EC:ECP], NPAD)
            V.memset(e_dst[:, EC:ECP], NPAD)
            V.memset(e_type[:, EC:ECP], 0).then_inc(pads, 1)
            V.memset(acc[:, (NT - 1) * D:NT * D], 0.0).then_inc(pads, 1)
            V.memset(ssq[:, :], 0.0)
            V.memset(braw, 0.0).then_inc(pads, 1)

            V.memset(ones[:, :], 1.0)
            V.memset(zeros[:, :], 0.0)
            V.memset(loc[:, 2 * LTD:2 * LTD + 4], -1.0)
            chain(V.memset(ssf[:, :], 0.0))
            dve.wait_ge(consts_i, 1)
            V.tensor_copy(iota_f[:, :], iota_i[:, 0:WIN // GT])
            V.tensor_copy(iota_h[:, :], iota_i[:, :])
            V.tensor_scalar(ident_h[:, :], dif[:, :], 0.0, None, ALU.is_equal)
            V.tensor_scalar(before[:, :], dif[:, :], 0.0, None, ALU.is_gt)
            V.tensor_copy(node1f[:, :], node1[:, :])
            V.tensor_scalar(invalid[:, :], node1[:, :], float(N), -100.0, ALU.is_gt, ALU.mult)
            V.tensor_scalar(ident[:, :], dif[:, :], 0.0, None, ALU.is_equal).then_inc(consts, 1)
            dve.wait_ge(consts, 1)

            dve.wait_ge(ld_edges, 48)

            def prepare(d):
                node, other = (e_src, e_dst) if d == 0 else (e_dst, e_src)
                a, b = e_tmp
                chain(V.tensor_scalar(a, node, 7, None, ALU.logical_shift_right))
                chain(V.tensor_copy(e_bin, a))
                chain(V.scalar_tensor_tensor(out=a, in0=e_type, scalar=float(NPAD), in1=other, op0=ALU.mult,
                                             op1=ALU.add))
                chain(V.tensor_scalar(b, a, 11, None, ALU.logical_shift_right))
                chain(V.tensor_scalar(e_pos.bitcast(I32), a, 2047, None, ALU.bitwise_and))
                chain(V.tensor_copy(e_lo[d], e_pos.bitcast(I32)))
                chain(V.tensor_scalar(a, node, P - 1, None, ALU.bitwise_and))
                chain(V.scalar_tensor_tensor(out=e_hi[d], in0=a, scalar=float(VROWS // 2048), in1=b, op0=ALU.mult,
                                             op1=ALU.add))
                chain(V.tensor_scalar(e_hi[d], e_hi[d], 1.0, None, ALU.add))
                chain(V.memset(e_pos, FAR))

            def edge_cols(d, blk):
                return slice(BLOCKS[d][blk][0], BLOCKS[d][blk][0] + BLOCKS[d][blk][1])

            def count_bins(m, d, b):
                for blk in range(2):
                    V.tensor_scalar((ind, scan)[blk][:, 0:BLOCKS[d][blk][1]], e_bin[:, edge_cols(d, blk)],
                                    iota_f[:, bass.ds(b, 1)], None, ALU.is_equal, ALU.add,
                                    accum_out=cnt[:, bass.ds(blk * NT + b, 1)]).then_inc(rank, 1)
                dve.wait_ge(rank, m + 2)

            def rank_bin(m, d, blk, b):
                cols, n = edge_cols(d, blk), BLOCKS[d][blk][1]
                V.tensor_scalar(ind[:, 0:n], e_bin[:, cols], iota_f[:, bass.ds(b, 1)], None,
                                ALU.is_equal).then_inc(rank, 1)
                dve.wait_ge(rank, m + 1)
                V.tensor_tensor_scan(scan[:, 0:n], ind[:, 0:n], zeros[:, 0:n], off[:, bass.ds(blk * NT + b, 1)],
                                     ALU.add, ALU.add).then_inc(rank, 1)
                dve.wait_ge(rank, m + 2)
                dve.nop(nofuse=True)
                V.copy_predicated(e_pos[:, cols], ind[:, 0:n].bitcast(I32), scan[:, 0:n]).then_inc(rank, 1)
                dve.wait_ge(rank, m + 3)

            def offsets(out0, bins_out, n_bins, wins, tiles):
                blocks, group = len(wins), float(tiles * P)
                dve.wait_ge(small_out, out0 + 1)
                chain(V.tensor_scalar(pre[:, 0:blocks * n_bins], ag[0][:, 0:blocks * n_bins], -1.0, None, ALU.add))
                t = tcol[0:n_bins, 0:blocks]
                chain(V.tensor_scalar(t, ag[1][0:n_bins, 0:blocks], (group - 1) / 2, 1.0 / group, ALU.add, ALU.mult))
                chain(V.tensor_scalar(t, t, RND, None, ALU.add))
                chain(V.tensor_scalar(t, t, -RND, None, ALU.add))
                for b in range(blocks):
                    cols = slice(b * n_bins, (b + 1) * n_bins)
                    V.tensor_scalar(tbc[0:n_bins, :], ones[0:n_bins, :], tcol[0:n_bins, b:b + 1], None,
                                    ALU.mult).then_inc(small_in, 1)
                    dve.wait_ge(small_out, out0 + 2 + 2 * b)
                    chain(V.scalar_tensor_tensor(out=off[:, cols], in0=ag[0][:, 0:n_bins], scalar=group,
                                                 in1=pre[:, cols], op0=ALU.mult, op1=ALU.add))
                    V.tensor_scalar(ge[0:n_bins, 0:wins[b]], iota_f[0:n_bins, 0:wins[b]], ag[1][0:n_bins, 0:1], None,
                                    ALU.is_ge).then_inc(small_in, 1)
                    dve.wait_ge(small_out, out0 + 3 + 2 * b)
                    chain(V.tensor_scalar(bins_out[:, sum(wins[:b]):sum(wins[:b + 1])], ag[2][0:1, 0:wins[b]], -1.0,
                                          None, ALU.add))

            def slot_places(pos, col, row, tmp=None):
                tmp = e_tmp[0].bitcast(F32)[:, 0:pos.shape[1]] if tmp is None else tmp
                chain(V.tensor_scalar(tmp, pos, -63.5, 1.0 / P, ALU.add, ALU.mult))
                chain(V.tensor_scalar(tmp, tmp, RND, None, ALU.add))
                chain(V.tensor_scalar(col, tmp, -RND, None, ALU.add))
                chain(V.scalar_tensor_tensor(out=row, in0=col, scalar=-float(P), in1=pos, op0=ALU.mult, op1=ALU.add))

            prepare(0)

            def norm_factors(at):
                V.tensor_scalar(ln[:, 0, :], mv[:, :, 1], 1e-5, None, ALU.add).then_inc(root, 1)
                dve.wait_ge(root, at + 2)
                chain(V.reciprocal(ln[:, 2, :], ln[:, 1, :]))
                chain(V.tensor_tensor(ln[:, 3, :], ln[:, 0, :], ln[:, 2, :], ALU.mult))
                chain(V.tensor_tensor(ln[:, 2, :], ln[:, 1, :], ln[:, 3, :], ALU.add))
                chain(V.tensor_scalar(ln[:, 3, :], ln[:, 2, :], 0.5, None, ALU.mult))
                chain(V.reciprocal(ln[:, 2, :], ln[:, 3, :]))
                V.tensor_scalar(ln[:, 5, :], ln[:, 2, :], YS, None, ALU.mult)
                chain(V.tensor_scalar(ln[:, 4, :], mv[:, :, 0], -1.0, None, ALU.mult))

            for g in range(ITS):
                dve.wait_ge(ld_x[g], 32 if g == ITS - 1 else 16)
                for j in range(STEPS * g, STEPS * (g + 1)):
                    last = V.bn_stats(st[:, j, :], acc[:, j * D:(j + 1) * D])
            chain(last)
            for j in range(NT):
                last = V.bn_aggr(mv[:, j, :], st[:, j, :])
            chain(last)
            norm_factors(0)

            def normed(n, u, tile, done):
                V.tensor_scalar(tile[:, u, :], acc[:, bass.ds(n * D, D)], ln[:, 4, bass.ds(n, 1)],
                                ln[:, 5, bass.ds(n, 1)], ALU.add, ALU.mult).then_inc(done, 1)

            def y_low(n, u):
                dve.wait_ge(yt_hi, n + 1)
                V.tensor_tensor(yT[:, 1, :, bass.ds(n * P, P)], pj[u % 2][:, :].rearrange("p (k n) -> p k n", k=DK),
                                yT[:, 0, :, bass.ds(n * P, P)], ALU.subtract).then_inc(yt_lo, 1)

            for n in range(2):
                normed(n, n, ytmp, y_ready)
            with dve.Fori(0, ITS - 1) as i:
                for u in range(STEPS):
                    normed(STEPS * i + u + 2, (u + 2) % 4, ytmp, y_ready)
                    count_bins(2 * (STEPS * i + u), 0, STEPS * i + u)
                    y_low(STEPS * i + u, u)
            for u in range(STEPS):
                if u < 2:
                    normed(NT - STEPS + u + 2, u + 2, ytmp, y_ready)
                count_bins(2 * (NT - STEPS + u), 0, NT - STEPS + u)
                y_low(NT - STEPS + u, u)
            dve.sem_inc(small_in, 1)
            offsets(0, lbin[:, 0:LTD // GT], NT, [w // GT for _, _, w in BLOCKS[0]], GT)

            def scales(total, e, extra=False):
                f = [e(c) for c in range(12)]
                chain(V.tensor_scalar(f[0].bitcast(F32), total, 1e-30, None, ALU.add))
                chain(V.tensor_scalar(f[1], f[0], 23, None, ALU.logical_shift_right))
                chain(V.tensor_scalar(f[2], f[1], 1.0, None, ALU.add))
                chain(V.tensor_scalar(f[4], f[2], 1, None, ALU.logical_shift_right))
                V.tensor_scalar(f[5], f[4], -1.0, 204.0, ALU.mult, ALU.add)
                V.tensor_scalar(f[8], f[4], 55.0, None, ALU.add)
                V.tensor_scalar(f[10], f[4], -1.0, 213.0, ALU.mult, ALU.add)
                chain(V.tensor_scalar(f[6], f[4], 41.0, None, ALU.add))
                V.tensor_scalar(f[3], f[5], 23, None, ALU.logical_shift_left)
                V.tensor_scalar(f[9], f[8], 23, None, ALU.logical_shift_left)
                V.tensor_scalar(f[11], f[10], 23, None, ALU.logical_shift_left)
                return V.tensor_scalar(f[7], f[6], 23, None, ALU.logical_shift_left)

            dve.wait_ge(squares, NW + 1)
            V.tensor_reduce(ssum[:, :], ssq[:, :], AX_X, ALU.add).then_inc(small_in, 1)
            dve.wait_ge(small_out, 6)
            chain(scales(ag[0][:, 0:1], lambda c: ex[:, c:c + 1]))
            dve.sem_inc(small_in, 1)
            w_scale = ex[:, 3:4].bitcast(F32)
            self_scale = ex[:, 7:8].bitcast(F32)
            agg_scale = ex[:, 9:10].bitcast(F32)
            def w_low(buf, c, q):
                dve.wait_ge(wt_hi, c + 1)
                V.scalar_tensor_tensor(
                    out=wmov[:, buf, 1].rearrange("p k n -> p (k n)")[:, bass.ds(q * D, D)], in0=wt[:, :],
                    scalar=w_scale, in1=wmov[:, buf, 0].rearrange("p k n -> p (k n)")[:, bass.ds(q * D, D)],
                    op0=ALU.mult, op1=ALU.subtract).then_inc(wt_lo, 1)

            for q in range(DK):
                w_low(0, q, q)

            def hot_codes(n, u, perm):
                d, cols, win = perm[0], *perm[4:6]
                back = 2 if len(cols) == 4 else (1, 3, 2)[u]
                dve.wait_ge(code_used, perm_step(perm, n, u) - back + 3)
                for v in range(cols[u]):
                    s = (u % 2) * 5 + v
                    f = perm_column(perm, n, u, v)
                    V.tensor_scalar(ohr[:, s, 0, :], iota_h[:, 0:P], e_row[d][:, bass.ds(f, 1)], None, ALU.is_equal)
                    last = V.tensor_scalar(ohc[:, s, 0:win], iota_h[:, 0:win], e_col[d][:, bass.ds(f, 1)], None,
                                           ALU.is_equal)
                last.then_inc(hot_ready, 1)

            def one_hots(i, vs):
                for v in vs:
                    t = LT * i + v
                    dve.wait_ge(agg, t + 1)
                    V.tensor_scalar(oh[:, v, :], iota_h[:, 0:P], loc[:, bass.ds(t, 1)], None,
                                    ALU.is_equal).then_inc(oh_ready, 1)

            def accumulate(i, vs):
                for v in vs[::GT]:
                    g = LT // GT * i + v // GT
                    j = dve.value_load(lbin[0:1, bass.ds(g, 1)], min_val=0, max_val=NT - 1)
                    tile = acc[:, bass.ds(j * D, D)]
                    dve.wait_ge(agg, LT * i + v + GT + LT)
                    dve.wait_ge(agg_read, g + 3)
                    V.scalar_tensor_tensor(out=tile, in0=ag[v // GT % 3][:, :], scalar=agg_scale, in1=tile,
                                           op0=ALU.mult, op1=ALU.add).then_inc(agg_read, 1)

            def row_low(w, q, u):
                dve.wait_ge(proj_hi, NT * w + STEPS * q + u + 1)
                V.scalar_tensor_tensor(out=trow[:, u, D:2 * D], in0=pj[u % 2][:, :], scalar=2.0 ** -14,
                                       in1=trow[:, u, 0:D], op0=ALU.mult, op1=ALU.subtract).then_inc(proj_read, 1)

            def iteration(w, par, q, perm, sort, chunk, summing):
                for u in range(STEPS):
                    b = STEPS * q + u
                    if perm and u < len(perm[4]):
                        hot_codes(ITS * (w - 1) + q, u, perm)
                    if summing:
                        one_hots(ITS * (w - R) + q - 1, PER_STEP[u])
                    if sort in ("rank 0, block 0", "rank 0, block 1"):
                        blk = int(sort == "rank 0, block 1")
                        rank_bin(2 * NT + 3 * (NT * blk + b), 0, blk, b)
                    if sort == "count 1":
                        count_bins(8 * NT + 2 * b, 1, b)
                    if sort in ("rank 1, block 0", "rank 1, block 1"):
                        blk = int(sort == "rank 1, block 1")
                        rank_bin(10 * NT + 3 * (NT * blk + b), 1, blk, b)
                    row_low(w, q, u)
                    if u == 2 and chunk:
                        w_low(1 - par, 4 * (w + 1) + q, q)
                    if summing:
                        accumulate(ITS * (w - R) + q - 1, PER_STEP[u])

            def relation(w, par, perm=None, sort=None, summing=False, lead=0):
                for q in range(lead):
                    iteration(w, par, q, perm, sort, True, False)
                with dve.Fori(lead, DK) as q:
                    iteration(w, par, q, perm, sort, True, summing)
                iteration(w, par, DK, perm, sort, False, summing)

            def decode(d, blk):
                dve.wait_ge(perm_done, 2 * d + blk + 1)
                win = BLOCKS[d][blk][2]
                start = d * LTD + blk * BLOCKS[d][0][2]
                hi, lo = pm[0][:, 0:win], pm[1][:, 0:win]
                whole, part = work[:, 0, 0:win], work[:, 1, 0:win]
                cols = slice(start, start + win)
                per = float(VROWS // 2048)
                V.tensor_scalar(whole, hi, -1.0, None, ALU.add)
                chain(V.tensor_scalar(part, hi, -1.0 - (per - 1) / 2, 1.0 / per, ALU.add, ALU.mult))
                chain(V.tensor_scalar(part, part, RND, None, ALU.add))
                chain(V.tensor_scalar(loc[:, cols], part, -RND, None, ALU.add))
                chain(V.scalar_tensor_tensor(out=part, in0=loc[:, cols], scalar=-per, in1=whole, op0=ALU.mult,
                                             op1=ALU.add))
                V.scalar_tensor_tensor(out=gidx[:, cols], in0=part, scalar=2048.0, in1=lo, op0=ALU.mult,
                                       op1=ALU.add).then_inc(lists, 1)

            def edge_places(d, blk):
                cols = slice(BLOCKS[d][blk][0], (BLOCKS[d][1][0], ECP)[blk])
                slot_places(e_pos[:, cols], e_col[d][:, cols], e_row[d][:, cols])

            relation(0, 0, sort="rank 0, block 0")
            edge_places(0, 0)
            relation(1, 1, PERMS[0], "rank 0, block 1")
            edge_places(0, 1)
            for w in range(2, 5):
                relation(w, w % 2, PERMS[0])
            prepare(1)
            relation(5, 1, PERMS[0], "count 1")
            dve.sem_inc(small_in, 1)
            offsets(6, lbin[:, LTD // GT:2 * LTD // GT], NT, [w // GT for _, _, w in BLOCKS[1]], GT)
            relation(6, 0, PERMS[0], "rank 1, block 0")
            relation(7, 1, PERMS[0], "rank 1, block 1")
            slot_places(e_pos, e_col[1], e_row[1])
            decode(0, 0)
            dve.wait_ge(acc_zero, 1)

            relation(8, 0, PERMS[1], summing=True, lead=1)
            for w in range(9, 12):
                relation(w, w % 2, PERMS[1], summing=True)
            decode(0, 1)
            with dve.Fori(0, 2) as pair:
                for par in range(2):
                    relation(2 * pair + par + 12, par, PERMS[2], summing=True)
            decode(1, 0)

            def self_step(b, slot, groups):
                tile = acc[:, bass.ds(b * D, D)]
                dve.wait_ge(proj, NT * SELF + b + 1)
                dve.wait_ge(agg_read, groups + 3)
                V.scalar_tensor_tensor(out=tile, in0=pj[slot][:, :], scalar=self_scale, in1=tile, op0=ALU.mult,
                                       op1=ALU.add).then_inc(proj_read, 1)
                dve.wait_ge(proj_read, NT * SELF + b + 3)

            def hots_ahead(i, u):
                one_hots(i + (u == STEPS - 1), PER_STEP[(u + 1) % STEPS])

            dve.wait_ge(code_used, perm_step(PERMS[3], PERMS[3][2], 0) + 2)
            for u in range(STEPS):
                hot_codes(PERMS[3][2], u, PERMS[3])
                if u % 2 == 0:
                    self_step(u // 2, u // 2, LTD // GT)
            one_hots(LIT, PER_STEP[0])
            with dve.Fori(1, SELF_ITS) as q:
                for u in range(STEPS):
                    hot_codes(PERMS[3][2] + q, u, PERMS[3])
                    hots_ahead(LIT + q - 1, u)
                    if u % 2 == 0:
                        self_step(2 * q + u // 2, u // 2, LT // GT * (LIT + q - 1) + PER_STEP[u][0] // GT)
                    accumulate(LIT + q - 1, PER_STEP[u])
            with dve.Fori(0, PERM_SUMS) as i:
                for u in range(STEPS):
                    hot_codes(PERMS[3][2] + SELF_ITS + i, u, PERMS[3])
                    hots_ahead(LIT + (SELF_ITS - 1) + i, u)
                    accumulate(LIT + (SELF_ITS - 1) + i, PER_STEP[u])
            decode(1, 1)

            rest = LIT + (SELF_ITS - 1) + PERM_SUMS
            base = steps[0]
            with dve.Fori(0, K_BINS) as k:
                for u in range(STEPS):
                    hots_ahead(rest + 2 * k, u)
                    accumulate(rest + 2 * k, PER_STEP[u])
                dve.wait_ge(small_out, 12 + k)
                steps[0] = base
                loop_at = [0]

                def chain_k(ins):
                    loop_at[0] += 1
                    ins.then_inc(step, 1)
                    dve.wait_ge(step, base + 5 * k + loop_at[0])

                f = [exf[:, c, bass.ds(k, 1)] for c in range(12)]
                chain_k(V.tensor_scalar(f[0].bitcast(F32), pj[0][:, bass.ds(k, 1)], 1e-30, None, ALU.add))
                chain_k(V.tensor_scalar(f[1], f[0], 23, None, ALU.logical_shift_right))
                chain_k(V.tensor_scalar(f[2], f[1], 1.0, None, ALU.add))
                chain_k(V.tensor_scalar(f[4], f[2], 1, None, ALU.logical_shift_right))
                V.tensor_scalar(f[5], f[4], -1.0, 204.0, ALU.mult, ALU.add)
                chain_k(V.tensor_scalar(f[6], f[4], 41.0, None, ALU.add))
                V.tensor_scalar(f[7], f[6], 23, None, ALU.logical_shift_left)
                V.tensor_scalar(f[3], f[5], 23, None, ALU.logical_shift_left).then_inc(small_in, 1)
                for u in range(STEPS):
                    hots_ahead(rest + 2 * k + 1, u)
                    accumulate(rest + 2 * k + 1, PER_STEP[u])
                dve.wait_ge(wf_hi, k + 1)
                V.scalar_tensor_tensor(out=wf[:, bass.ds(4096 * k + 2048, 2048)], in0=wfraw,
                                       scalar=f[3].bitcast(F32), in1=wf[:, bass.ds(4096 * k, 2048)],
                                       op0=ALU.mult, op1=ALU.subtract).then_inc(wf_lo, 1)
            steps[0] = base + 5 * K_BINS
            with dve.Fori(rest + 2 * K_BINS, 2 * LIT) as i:
                for u in range(STEPS):
                    hots_ahead(i, u)
                    accumulate(i, PER_STEP[u])

            dve.wait_ge(agg_read, 2 * LTD // GT + 3)
            with dve.Fori(0, ITS) as i:
                for u in range(STEPS + 1):
                    if u < STEPS:
                        tile = acc[:, bass.ds((STEPS * i + u) * D, D)]
                        dve.wait_ge(ld_x2[u], 16 * (i + 1))
                        V.scalar_tensor_tensor(out=tile, in0=tile, scalar=0.0, in1=xin[:, u, :], op0=ALU.max,
                                               op1=ALU.add).then_inc(x1_done, 1)
                    if u:
                        j = STEPS * i + u - 1
                        dve.wait_ge(x1_done, j + 1)
                        last = V.bn_stats(st[:, bass.ds(j, 1), :].rearrange("p a s -> p (a s)"),
                                          acc[:, bass.ds(j * D, D)])
            chain(V.memset(fb[:, 3, :], FAR))
            for j in range(NT):
                last = V.bn_aggr(mv[:, j, :], st[:, j, :])
            chain(last)
            norm_factors(2)
            V.tensor_tensor(ln[:, 2, :], ln[:, 4, :], ln[:, 5, :], ALU.mult).then_inc(f_norm, 1)

            xcol = acc[:, :].rearrange("p (t d) -> p t d", t=NT)[:, :, 0]
            chain(V.tensor_tensor(fb[:, 0, :], xcol, ln[:, 4, :], ALU.add))
            chain(V.tensor_tensor(fb[:, 0, :], fb[:, 0, :], ln[:, 5, :], ALU.mult))
            chain(V.tensor_copy(fb[:, 1, :], invalid[:, :]))
            for edge in BINS:
                chain(V.scalar_tensor_tensor(out=fb[:, 1, :], in0=fb[:, 0, :], scalar=edge * YS, in1=fb[:, 1, :],
                                             op0=ALU.is_gt, op1=ALU.add))
            for b in range(K_BINS):
                chain(V.tensor_scalar(fb[:, 2, :], fb[:, 1, :], float(b), None, ALU.is_equal, ALU.add,
                                      accum_out=cnt[:, b:b + 1]))
            dve.sem_inc(small_in, 1)
            offsets(19, fbin, K_BINS, [FT], 1)
            for b in range(K_BINS):
                chain(V.tensor_scalar(fb[:, 2, :], fb[:, 1, :], float(b), None, ALU.is_equal))
                chain(V.tensor_tensor_scan(fb[:, 4, :], fb[:, 2, :], zeros[:, 0:NT], off[:, b:b + 1], ALU.add,
                                           ALU.add))
                chain(V.copy_predicated(fb[:, 3, :], fb[:, 2, :].bitcast(I32), fb[:, 4, :]))
            slot_places(fb[:, 3, :], fb[:, 5, :], fb[:, 6, :], fb[:, 7, :])
            for n in range(NT):
                if n >= 4:
                    dve.wait_ge(f_used, n - 3)
                V.tensor_scalar(fsc[:, n % 4, :], iota_f[:, 0:FT], fb[:, 5, n:n + 1], None, ALU.is_equal)
                V.tensor_scalar(fsa[:, n % 4, :], iota_f[:, 0:P], fb[:, 6, n:n + 1], node1f[:, n:n + 1],
                                ALU.is_equal, ALU.mult).then_inc(f_code, 1)
            dve.wait_ge(f_used, NT)
            chain(V.tensor_scalar(fd[:, 0, :], pm[0][:, 0:FT], -1.0, None, ALU.add))
            V.tensor_scalar(fgi[:, :], fd[:, 0, :], 0.0, None, ALU.max)
            chain(V.tensor_scalar(fd[:, 1, :], fd[:, 0, :], 0.0, float(2 ** 20), ALU.is_lt, ALU.mult))
            V.tensor_tensor(fsi[:, :], fd[:, 1, :], fd[:, 0, :], ALU.add).then_inc(f_idx, 1)

            def f_sum(i, u, reused):
                    t = 4 * i + u
                    kb = dve.value_load(fbin[0:1, bass.ds(t, 1)], min_val=0, max_val=K_BINS - 1)
                    dve.wait_ge(f_mm, t + 1)
                    if reused:
                        dve.wait_ge(f_out[u], 16 * i)
                    V.scalar_tensor_tensor(out=fout[:, u, :], in0=ag[u % 2][:, :],
                                           scalar=exf[:, 7, bass.ds(kb, 1)].bitcast(F32),
                                           in1=frow[:, u, 2 * D:4 * D].bitcast(F32), op0=ALU.mult,
                                           op1=ALU.add).then_inc(f_add, 1)

            for u in range(4):
                f_sum(0, u, False)
            with dve.Fori(1, FT // 4) as i:
                for u in range(4):
                    f_sum(i, u, True)


_INS = ['x', 'src', 'dst', 'edge_type_8', 'L0_gnn_W_self', 'L0_gnn_b_self', 'L0_gnn_W_rel', 'L0_gnn_b_rel', 'L0_ffn_W']


def kernel(**inputs):
    import numpy as _np
    import concourse.bacc as _bacc
    from concourse import mybir as _mybir
    from concourse.bass_utils import run_bass_kernel_spmd as _run

    nc = _bacc.Bacc("TRN2", target_bir_lowering=False, num_devices=1)
    arrays, args = {}, []
    for name in _INS:
        a = _np.ascontiguousarray(inputs[name])
        arrays[f"in_{name}"] = a
        args.append(nc.dram_tensor(f"in_{name}", a.shape, _mybir.dt.from_np(a.dtype), kind="ExternalInput").ap())
    out = nc.dram_tensor("out_0", (N, D), _mybir.dt.float32, kind="ExternalOutput").ap()
    build(nc, *args, out)
    r = _run(nc, [arrays], core_ids=[0])
    return r.results[0]["out_0"]
```
